# Optimizing a Trainium2 kernel written in Bass

```python
import numpy as np
import jax
import jax.numpy as jnp

def _softmax(x, axis=-1):
    return jax.nn.softmax(x, axis=axis)

def _gelu(x):
    return jax.nn.gelu(x, approximate=True)

def _silu(x):
    return jax.nn.silu(x)

def _sigmoid(x):
    return jax.nn.sigmoid(x)

def _layernorm(x, axis=-1, eps=1e-05):
    m = jnp.mean(x, axis=axis, keepdims=True)
    v = jnp.var(x, axis=axis, keepdims=True)
    return (x - m) / jnp.sqrt(v + eps)

def _scatter_add(tgt, idx, src, axis=0):
    return tgt.at[idx].add(src)

def _segment_sum(src, seg, n):
    return jax.ops.segment_sum(src, seg, n)
kernel_name = 'mk_audio_tower_d1_tok_audfeat256_r4_702e3c'

def setup_inputs(seed: int=0):
    np.random.seed(seed)
    _w = jnp.asarray

    def _rec_inputs():
        import jax
        import jax.numpy as jnp
        _rk = jax.random.key(seed)
        x = 7.22013e-05 + 1.00017 * jax.random.normal(jax.random.fold_in(_rk, 1), (16, 256, 64), jnp.float32)
        return x
    x = _rec_inputs()

    def _L0_tok_setup():
        import jax, jax.numpy as jnp
        import numpy as np
        WIN = 9
        key = jax.random.key(seed)
        ks = jax.random.split(key, 4)
        N, L, C, U = (8, 1024, 64, 64)
        x = jax.random.normal(ks[0], (N, L, C), dtype=jnp.float32)
        W_qry = jax.random.normal(ks[1], (C, U), dtype=jnp.float32) * 0.05
        W_key = jax.random.normal(ks[2], (C, U), dtype=jnp.float32) * 0.05
        v = jax.random.normal(ks[3], (U,), dtype=jnp.float32) * 0.05
        b = jnp.zeros((U,), dtype=jnp.float32)
        return {'x': x, 'W_qry': W_qry, 'W_key': W_key, 'v': v, 'b': b}
    _L0_tok_all = _L0_tok_setup()
    _L0_tok_in = {k: v for k, v in _L0_tok_all.items() if k in ('W_qry', 'W_key', 'v', 'b')}
    del _L0_tok_all

    def _L0_attn_setup():
        import jax, jax.numpy as jnp
        import numpy as np
        D_MODEL = 64
        N_HEAD = 8

        def _l1_scores(q, k):
            scale = 1.0 / np.sqrt(q.shape[-1]).astype(np.float32)
            q_sbhw = q.transpose(1, 0, 2, 3)

            def one_query(qs):
                return -jnp.sum(jnp.abs(qs[:, None, :, :] - k), axis=-1) * scale
            s = jax.lax.map(one_query, q_sbhw)
            return s.transpose(1, 0, 2, 3)
        key = jax.random.key(seed)
        ks = jax.random.split(key, 3)
        b, t = (4, 250)
        x = jax.random.normal(ks[0], (b, t, D_MODEL), jnp.float32)
        wqv_w = 0.005 * jax.random.normal(ks[1], (3 * N_HEAD * D_MODEL, D_MODEL), jnp.float32)
        wqv_b = jnp.zeros((3 * N_HEAD * D_MODEL,), jnp.float32)
        wk = 0.005 * jnp.ones((N_HEAD, D_MODEL), jnp.float32)
        fanin_w = 0.005 * jax.random.normal(ks[2], (D_MODEL, D_MODEL), jnp.float32)
        fanin_b = jnp.zeros((D_MODEL,), jnp.float32)
        return dict(x=x, wqv_w=wqv_w, wqv_b=wqv_b, wk=wk, fanin_w=fanin_w, fanin_b=fanin_b)
    _L0_attn_all = _L0_attn_setup()
    _L0_attn_in = {k: v for k, v in _L0_attn_all.items() if k in ('wqv_w', 'wqv_b', 'wk', 'fanin_w', 'fanin_b')}
    del _L0_attn_all

    def _L0_ffn_setup():
        import jax, jax.numpy as jnp
        import numpy as np
        DIM = 64
        HEADS = 8
        NUM_KEYS = 64
        NUM_KV = NUM_KEYS ** 2
        PK_TOPK = 16
        FINAL_TOPK = 16
        DIM_KEY = DIM // 2
        P = 2

        def _pk(x, Wq_pk, pk_keys):
            b, n, _ = x.shape
            q = (x @ Wq_pk).reshape(b, n, P, HEADS, DIM_KEY).transpose(2, 0, 1, 3, 4)
            sim = jnp.einsum('pbnhd,pkhd->pbnhk', q, pk_keys)
            scores, idx = jax.lax.top_k(sim, PK_TOPK)
            idx0 = idx[0]
            idx1 = idx[1] * NUM_KEYS
            index = (idx0[..., :, None] + idx1[..., None, :]).reshape(b, n, HEADS, PK_TOPK * PK_TOPK)
            score = (scores[0][..., :, None] + scores[1][..., None, :]).reshape(b, n, HEADS, PK_TOPK * PK_TOPK)
            final_scores, pk_idx = jax.lax.top_k(score, FINAL_TOPK)
            final_indices = jnp.take_along_axis(index, pk_idx, axis=-1)
            final_scores = jax.nn.softmax(final_scores, axis=-1)
            return (final_scores, final_indices)
        key = jax.random.key(seed)
        ks = jax.random.split(key, 7)
        b, n = (2, 256)
        std = 0.02
        x = jax.random.normal(ks[0], (b, n, DIM), dtype=jnp.float32)
        Wq_pk = jax.random.normal(ks[1], (DIM, P * HEADS * DIM_KEY), dtype=jnp.float32) * std
        pk_keys = jax.random.normal(ks[2], (P, NUM_KEYS, HEADS, DIM_KEY), dtype=jnp.float32) * std
        Wq = jax.random.normal(ks[3], (DIM, HEADS * DIM), dtype=jnp.float32) * std
        keys_table = jax.random.normal(ks[4], (NUM_KV * HEADS, DIM), dtype=jnp.float32) * std
        values_table = jax.random.normal(ks[5], (NUM_KV * HEADS, DIM), dtype=jnp.float32) * std
        Wo = jax.random.normal(ks[6], (DIM * HEADS, DIM), dtype=jnp.float32) * std
        return {'x': x, 'Wq_pk': Wq_pk, 'pk_keys': pk_keys, 'Wq': Wq, 'keys_table': keys_table, 'values_table': values_table, 'Wo': Wo}
    _L0_ffn_all = _L0_ffn_setup()
    _L0_ffn_in = {k: v for k, v in _L0_ffn_all.items() if k in ('Wq_pk', 'pk_keys', 'Wq', 'keys_table', 'values_table', 'Wo')}
    del _L0_ffn_all
    return {'x': x, 'L0_tok_W_qry': _L0_tok_in['W_qry'], 'L0_tok_W_key': _L0_tok_in['W_key'], 'L0_tok_v': _L0_tok_in['v'], 'L0_tok_b': _L0_tok_in['b'], 'L0_attn_wqv_w': _L0_attn_in['wqv_w'], 'L0_attn_wqv_b': _L0_attn_in['wqv_b'], 'L0_attn_wk': _L0_attn_in['wk'], 'L0_attn_fanin_w': _L0_attn_in['fanin_w'], 'L0_attn_fanin_b': _L0_attn_in['fanin_b'], 'L0_ffn_Wq_pk': _L0_ffn_in['Wq_pk'], 'L0_ffn_pk_keys': _L0_ffn_in['pk_keys'], 'L0_ffn_Wq': _L0_ffn_in['Wq'], 'L0_ffn_keys_table': _L0_ffn_in['keys_table'], 'L0_ffn_values_table': _L0_ffn_in['values_table'], 'L0_ffn_Wo': _L0_ffn_in['Wo']}

def reference(x, L0_tok_W_qry, L0_tok_W_key, L0_tok_v, L0_tok_b, L0_attn_wqv_w, L0_attn_wqv_b, L0_attn_wk, L0_attn_fanin_w, L0_attn_fanin_b, L0_ffn_Wq_pk, L0_ffn_pk_keys, L0_ffn_Wq, L0_ffn_keys_table, L0_ffn_values_table, L0_ffn_Wo):
    import jax
    import jax.numpy as jnp

    def _L0_tok_ref(x, W_qry, W_key, v, b):
        import jax, jax.numpy as jnp
        import numpy as np
        WIN = 9
        N, L, C = x.shape
        n_w = L - WIN + 1
        idx = jnp.arange(n_w)[:, None] + jnp.arange(WIN)[None, :]
        x_win = x[:, idx]
        x_ctr = x[:, WIN // 2:WIN // 2 + n_w]
        key = jnp.einsum('nwsc,cu->nwsu', x_win, W_key)
        qry = jnp.einsum('nwc,cu->nwu', x_ctr, W_qry)
        score = jnp.einsum('nwsu,u->nws', jnp.tanh(qry[:, :, None, :] + key + b), v)
        weight = jax.nn.softmax(score, axis=2)
        out = jnp.einsum('nwsc,nws->nwc', x_win, weight)
        return out

    def _L0_attn_ref(x, wqv_w, wqv_b, wk, fanin_w, fanin_b):
        import jax, jax.numpy as jnp
        import numpy as np
        D_MODEL = 64
        N_HEAD = 8

        def _l1_scores(q, k):
            scale = 1.0 / np.sqrt(q.shape[-1]).astype(np.float32)
            q_sbhw = q.transpose(1, 0, 2, 3)

            def one_query(qs):
                return -jnp.sum(jnp.abs(qs[:, None, :, :] - k), axis=-1) * scale
            s = jax.lax.map(one_query, q_sbhw)
            return s.transpose(1, 0, 2, 3)
        b, t, d = x.shape
        h = N_HEAD
        v = (x @ wqv_w.T + wqv_b).reshape(b, t, 3 * h, d)
        q, vf, vb = (v[:, :, :h], v[:, :, h:2 * h], v[:, :, 2 * h:])
        k = x[:, :, None, :] * wk[None, None]
        a = _l1_scores(q, k)
        a = jnp.concatenate([a, jnp.zeros((b, 1, t, h), a.dtype)], axis=1)
        a = jax.nn.softmax(a, axis=1)[:, :t]
        bf = jnp.einsum('bsdh,bshw->bdhw', a, vf)
        bb = jnp.einsum('bdsh,bshw->bdhw', a, vb)
        o = (bf + bb).sum(axis=2).reshape(b, t, d)
        y = o * jax.nn.sigmoid(1.702 * o)
        y = y @ fanin_w.T + fanin_b
        return x + y

    def _L0_ffn_ref(x, Wq_pk, pk_keys, Wq, keys_table, values_table, Wo):
        import jax, jax.numpy as jnp
        import numpy as np
        DIM = 64
        HEADS = 8
        NUM_KEYS = 64
        NUM_KV = NUM_KEYS ** 2
        PK_TOPK = 16
        FINAL_TOPK = 16
        DIM_KEY = DIM // 2
        P = 2

        def _pk(x, Wq_pk, pk_keys):
            b, n, _ = x.shape
            q = (x @ Wq_pk).reshape(b, n, P, HEADS, DIM_KEY).transpose(2, 0, 1, 3, 4)
            sim = jnp.einsum('pbnhd,pkhd->pbnhk', q, pk_keys)
            scores, idx = jax.lax.top_k(sim, PK_TOPK)
            idx0 = idx[0]
            idx1 = idx[1] * NUM_KEYS
            index = (idx0[..., :, None] + idx1[..., None, :]).reshape(b, n, HEADS, PK_TOPK * PK_TOPK)
            score = (scores[0][..., :, None] + scores[1][..., None, :]).reshape(b, n, HEADS, PK_TOPK * PK_TOPK)
            final_scores, pk_idx = jax.lax.top_k(score, FINAL_TOPK)
            final_indices = jnp.take_along_axis(index, pk_idx, axis=-1)
            final_scores = jax.nn.softmax(final_scores, axis=-1)
            return (final_scores, final_indices)
        b, n, d = x.shape
        q = (x @ Wq).reshape(b, n, HEADS, DIM) * DIM ** (-0.5)
        kv_scores, indices = _pk(x, Wq_pk, pk_keys)
        offsets = jnp.arange(HEADS, dtype=indices.dtype) * NUM_KV
        ind = indices + offsets[None, None, :, None]
        k = jnp.einsum('bnhk,bnhkd->bnhd', kv_scores, keys_table[ind])
        v = jnp.einsum('bnhk,bnhkd->bnhd', kv_scores, values_table[ind])
        sim = jnp.einsum('bihd,bjhd->bhij', q, k)
        neg = -jnp.finfo(sim.dtype).max
        causal = jnp.tril(jnp.ones((n, n), dtype=bool))
        sim = jnp.where(causal, sim, neg)
        attn = jax.nn.softmax(sim, axis=-1)
        out = jnp.einsum('bhij,bjhd->bhid', attn, v)
        out = out.transpose(0, 2, 1, 3).reshape(b, n, HEADS * DIM)
        return out @ Wo
    h = _L0_tok_ref(x, L0_tok_W_qry, L0_tok_W_key, L0_tok_v, L0_tok_b)
    h = h + _L0_attn_ref(_layernorm(h, axis=-1), L0_attn_wqv_w, L0_attn_wqv_b, L0_attn_wk, L0_attn_fanin_w, L0_attn_fanin_b)
    h = h + _L0_ffn_ref(_layernorm(h, axis=-1), L0_ffn_Wq_pk, L0_ffn_pk_keys, L0_ffn_Wq, L0_ffn_keys_table, L0_ffn_values_table, L0_ffn_Wo)
    return h

_drawn_inputs = setup_inputs


def setup_inputs(seed=0):
    import zlib

    import numpy as np

    out = dict(_drawn_inputs(seed))
    spreads = {'L0_tok_b': (0.0, 0.8),
     'L0_attn_wqv_b': (0.0, 0.8),
     'L0_attn_wk': (0.004999999888241291, 0.6),
     'L0_attn_fanin_b': (0.0, 0.1)}
    factors = {'L0_attn_wqv_w': 8.0,
     'L0_attn_fanin_w': 8.0,
     'L0_ffn_Wq_pk': 8.0,
     'L0_ffn_pk_keys': 8.0,
     'L0_ffn_Wq': 64.0,
     'L0_ffn_keys_table': 64.0,
     'L0_ffn_values_table': 8.0,
     'L0_ffn_Wo': 8.0}
    for name, (base, spread) in spreads.items():
        noise = np.random.default_rng([zlib.crc32(name.encode()), seed]).standard_normal(out[name].shape)
        drawn = base * np.exp(spread * noise) if base else spread * noise
        out[name] = jnp.asarray(drawn.astype(out[name].dtype))
    for name, factor in factors.items():
        out[name] = (out[name] * factor).astype(out[name].dtype)
    return out
```

```python
from contextlib import ExitStack

import numpy as np

import concourse.bass as bass
from concourse import mybir

F32 = mybir.dt.float32
U32 = mybir.dt.uint32
ALU = mybir.AluOpType
ACT = mybir.ActivationFunctionType
AX = mybir.AxisListType

P = 128
NB, L, C = 16, 256, 64
WIN = 9
NW = L - WIN + 1
PAIRS = NB // 2
HT = NW // 2
H = 8
GR = 4
STEPS = 16
BT = GR * STEPS
BLOCKS = 4
RING = 2
NK = 64
TOP = 16
TIES = [(0, 1, 16), (1, 1, 8), (2, 3, 5), (5, 3, 2), (8, 8, 1)]
CAND = sum(n * m for _, n, m in TIES)
EPS = 1e-5
TINY = 1e-20
SLOTS = 4
UNITS = 4 * H
LOWEST = -3.0e38
MASKED = -1.0e30

C_ID, C_MASK, C_ROWS, C_IOTA, C_HOFF = 0, 128, 376, 384, 384 + CAND
C_END = C_HOFF + H * TOP


def constants():
    c = np.zeros((P, C_END), np.float32)
    c[:, C_ID:C_ID + P] = np.eye(P)
    i, j = np.arange(HT)[:, None], np.arange(HT)[None, :]
    c[:HT, C_MASK + HT:C_MASK + 2 * HT] = np.where(j <= i, 0.0, MASKED)
    r = np.arange(P)
    g, b, s = r // 32, r // 16 % 2, r % 16
    for k in range(BLOCKS):
        t = k * BT + g * STEPS + s
        for bb in range(2):
            c[:, C_ROWS + 2 * k + bb] = (b == bb) & (t < NW)
    c[:, C_IOTA:C_IOTA + CAND] = np.arange(CAND)
    c[:, C_HOFF:C_END] = np.repeat(np.arange(H) * NK * NK, TOP)
    return c


class Chain:

    def __init__(self, eng, sem, per, passed=None):
        self.eng, self.sem, self.per, self.passed = eng, sem, per, passed

    def begin(self, instance):
        self.base, self.n = instance * self.per, 0

    def link(self, ins):
        self.n += 1
        ins.then_inc(self.sem, 1)

    def wait(self):
        self.eng.wait_ge(self.sem, self.base + self.n)

    def hold(self):
        self.wait()
        self.eng.sem_inc(self.passed, 1)

    def step(self, ins):
        self.link(ins)
        self.wait()

    def end(self):
        assert self.n == self.per, (self.sem, self.n)


TOK_LINKS, PREP_LINKS, BLK_LINKS, POST_LINKS, TOPK_LINKS, SUM_LINKS, CAUSAL_LINKS = 13, 14, 13, 8, 142, 1, 64
SETUP_LINKS = 25

FILL5_TOK, FILL5_BLK, FILL5_POST, FILL5_TOPK = 0, 2, 2 + 3 * BLOCKS, 3 + 3 * BLOCKS
FILLS5 = FILL5_TOPK + 4
FILL6_TOK, FILL6_PREP, FILL6_BLK, FILL6_POST, FILL6_TOPK = 0, 1, 2, 2 + 3 * BLOCKS, 3 + 3 * BLOCKS
FILLS6 = FILL6_TOPK + 4
CREDITED = ("tok_done", "kv_done", "bank5_read", "bank6_read", "exps_done", "av_ready", "topk_done", "v_ready",
            "ot_added", "stored", "c_read")
CAUSAL_FILLS = 8 + 4 * (3 * 4 + 1)


def build(nc, x, xT, w_qry, w_key, v_tok, b_tok, wqvT, bqT, b_qv, wkT, faninT, b_fanin,
          wpkT, pkT, wq, tables, wo, consts, out):
    with ExitStack() as ctx:
        def sb(name, shape, dt=F32):
            return ctx.enter_context(nc.sbuf_tensor(name, shape, dt))

        def sem(name):
            return ctx.enter_context(nc.semaphore(name))

        psum = ctx.enter_context(nc.psum_tensor("psum", [P, 8, 512], F32))

        con = sb("con", [P, C_END])
        wkey2, wqry2 = sb("wkey2", [P, P]), sb("wqry2", [P, P])
        tokb = sb("tokb", [P, 1])
        vblk = sb("vblk", [P, 2])
        wqh = sb("wqh", [P, H, P])
        bq = sb("bq", [P, H])
        wkt = sb("wkt", [P, H])
        wk_s = sb("wk_s", [P, 5, H])
        wvf = sb("wvf", [P, H, 2, C])
        wvb = sb("wvb", [P, H * C])
        bvf, bvb = sb("bvf", [P, H * C]), sb("bvb", [P, H * C])
        fb = sb("fb", [P, C])
        fan2 = sb("fan2", [P, P])
        wq2 = sb("wq2", [P, H, P])
        wo_sb = sb("wo_sb", [P, 4, C])
        wc = sb("wc", [P, 2 * H * NK])
        wpat = sb("wpat", [P, H, 47])
        acor = sb("acor", [P, H, GR, 2, STEPS])

        xt = sb("xt", [P, L])
        qry, key = sb("qry", [P, NW]), sb("key", [P, L])
        sc = sb("sc", [HT, 4, WIN])
        small = sb("small", [P, 12, 8])
        h1, x1, hx = sb("h1", [HT, 4, C]), sb("x1", [HT, 4, C]), sb("hx", [HT, 4, C])
        h2, x2 = sb("h2", [HT, 4, C]), sb("x2", [HT, 4, C])
        cen, sq = sb("cen", [HT, 4, C]), sb("sq", [HT, 4, C])
        x1t, nx1t = sb("x1t", [P, BLOCKS * BT]), sb("nx1t", [P, BLOCKS * BT])
        qp = sb("qp", [P, H, NW])
        vf = sb("vf", [HT, 2, H * P])
        x2k = sb("x2k", [P, GR, 2, STEPS])
        bt = sb("bt", [P, H])
        vbs = sb("vbs", [P, H, 2, C])
        e = sb("e", [P, H, NW])
        z = sb("z", [P, 3, H])
        at = sb("at", [P, 2 * H, P])
        ot, og, th = sb("ot", [P, BLOCKS * BT]), sb("og", [P, NW]), sb("th", [P, NW])
        x2t = sb("x2t", [P, NW])
        tv, ti = sb("tv", [HT, 2, H, TOP]), sb("ti", [HT, 2, H, TOP], U32)
        code = sb("code", [HT, 2, H, TOP])
        fv, fi, ff = sb("fv", [HT, H, TOP]), sb("fi", [HT, H, TOP], U32), sb("ff", [HT, H, TOP])
        keyf = sb("keyf", [HT, H, TOP])
        idx = sb("idx", [HT, 2, H, 2, TOP], U32)
        wt = sb("wt", [HT, 2, H, 2, TOP])
        g_rows = sb("g_rows", [HT, SLOTS, TOP, 2 * C])
        kv = sb("kv", [HT, 2, H, 2, 2, C])
        outb = sb("outb", [HT, 4, C])

        ring = sb("ring", [P, RING * GR * H * NW])
        d = ring[:, :].rearrange("p (q g n) -> p q g n", q=RING, g=GR)
        at_ = [0]

        def part(n, rows=P):
            a = ring[0:rows, at_[0]:at_[0] + n]
            at_[0] += n
            return a
        zt = part(WIN * NW)
        xw = part(4 * WIN * C, HT)
        sim = part(2 * H * NK, HT)
        cs = part(H * CAND, HT).rearrange("p (h c) -> p h c", h=H)
        cc = part(H * CAND, HT).rearrange("p (h c) -> p h c", h=H)
        eq = part(4 * TOP * CAND, HT)
        qt = part(H * NW).rearrange("p (h n) -> p h n", h=H)
        kt = part(H * NW).rearrange("p (h n) -> p h n", h=H)
        sm = part(2 * NW, HT)
        pt = part(4 * HT, HT).rearrange("p (a n) -> p a n", a=4)
        ott = part(4 * HT).rearrange("p (a n) -> p a n", a=4)
        assert at_[0] <= RING * GR * H * NW
        wpk_sb = ring[:, 0:4 * P].rearrange("p (g c) -> p g c", g=4)
        pkb = ring[:, 4 * P:4 * P + 4 * 4 * NK].rearrange("p (g h k) -> p g h k", g=4, h=4)
        v1 = at[:, 0:4, :].rearrange("p a (b w) -> p (a b) w", w=C)

        ident = con[:, C_ID:C_ID + P]
        S = psum[:, 0:4, 0:2 * NW].rearrange("p k (h n) -> p k h n", h=2)

        def s_of(h, rows=slice(0, P)):
            return S[rows, h // 2, h % 2, :]

        b4, b5, b6, b7 = (psum[:, k, :] for k in (4, 5, 6, 7))

        names = """zeroed w_loaded setup_dve setup_wc wc_ready setup_done
            x_loaded tok_proj tok_z tok_tanh tok_scores tok_sub tok_exp tok_var tok_sqrt tok_dve tok_done x1_done
            x1t_ready prep_done q_ready q_read vf_ready vf_done prep_dve
            x2k_ready v_ready v_done quad_act quad_dve quad_free s_ready exps_done attn_norm at_filled at_copied
            av_ready ot_added blk_dve
            o_tanh og_ready y_ready post_var post_sqrt x2_done x2t_ready x2t_done post_dve
            sims_ready sims_copied topk_done fin_sub fin_exp idx_ready topk_dve
            bank5_read bank6_read dve_passed pool_passed sp_passed
            slot_free kv_done sum_dve
            c_filled c_read c_exp c_neg c_norm c_out c_dve stored""".split()
        s = {n: sem(n) for n in names}
        loaded = [sem(f"slot{i}_loaded") for i in range(SLOTS)]

        ZEROS = 8
        both = [slice(0, C), slice(C, 2 * C)]
        wd = [(con[:, :], consts)]
        for b, r in enumerate(both):
            wd += [(wkey2[r, r], w_key), (wqry2[r, r], w_qry), (tokb[r, :], b_tok.unsqueeze(1)),
                   (vblk[r, b:b + 1], v_tok.unsqueeze(1)),
                   (wqh[r, :, r], wqvT[:, 0:512].rearrange("c (h w) -> c h w", h=H)),
                   (bq[r, :], bqT), (wkt[r, :], wkT),
                   (wvf[r, :, b, :], wqvT[:, 512:1024].rearrange("c (h w) -> c h w", h=H)),
                   (wvb[r, :], wqvT[:, 1024:1536]), (fan2[r, r], faninT),
                   (wq2[r, :, r], wq.rearrange("c (h w) -> c h w", h=H)),
                   (wpk_sb[:, :, r], wpkT.rearrange("g p c -> p g c"))]
        wd += [(bvf[:, :], b_qv[512:1024].partition_broadcast(P)),
               (bvb[:, :], b_qv[1024:1536].partition_broadcast(P)),
               (fb[:, :], b_fanin.partition_broadcast(P)),
               (wo_sb[:, :, :], wo.rearrange("(a p) n -> p a n", p=P))]
        wd += [(pkb[32 * a:32 * a + 32, :, a, :], pkT[:, 32 * a:32 * a + 32, :].rearrange("g p k -> p g k"))
               for a in range(4)]

        block = ctx.enter_context(nc.Block())

        @block.sync
        def _(sp):
            sp.wait_ge(s["zeroed"], ZEROS)
            for dst, src in wd:
                sp.dma_start(dst, src).then_inc(s["w_loaded"], 16)
            sp.wait_ge(s["setup_done"], 1)
            with sp.Fori(0, PAIRS) as p:
                sp.wait_ge(s["tok_done"], p + 1)
                sp.wait_ge(s["kv_done"], p * UNITS + 1)
                sp.sem_inc(s["sp_passed"], 1)
                sp.dma_start(xt[:, :], xT[bass.ds(p, 1), :, :].rearrange("a p l -> p (a l)"))\
                    .then_inc(s["x_loaded"], 16)
                for hb in range(4):
                    half, b = hb // 2, hb % 2
                    src = bass.AP(x.tensor, p * (2 * L * C) + (b * L + half * HT) * C, [[C, HT], [1, WIN * C]])
                    sp.dma_start(xw[:, hb * WIN * C:(hb + 1) * WIN * C], src).then_inc(s["x_loaded"], 16)
                for t in range(4):
                    sp.wait_ge(s["c_out"], 4 * p + t + 1)
                    sp.sem_inc(s["sp_passed"], 1)
                    b, half = t // 2, t % 2
                    sp.dma_start(out[bass.ds(2 * p + b, 1), half * HT:(half + 1) * HT, :]
                                 .rearrange("a t c -> (a t) c"), outb[:, t, :]).then_inc(s["stored"], 16)
            sp.wait_ge(s["stored"], 16 * 4 * PAIRS + 1)

        @block.gpsimd
        def _(pool):
            pool.wait_ge(s["setup_done"], 1)
            with pool.Fori(0, PAIRS) as p:
                for half in range(2):
                    pool.wait_ge(s["idx_ready"], 4 * p + 2 * half + 2)
                    for v in range(2 * H):
                        h, b = v // 2, v % 2
                        u = half * 2 * H + v
                        pool.wait_ge(s["slot_free"], p * UNITS + u + 1)
                        pool.sem_inc(s["pool_passed"], 1)
                        for m in range(TOP):
                            nc.gpsimd.indirect_dma_start(
                                g_rows[:, u % SLOTS, m, :], None, tables,
                                bass.IndirectOffsetOnAxis(idx[:, half, h, b, m:m + 1], 0))\
                                .then_inc(loaded[u % SLOTS], 16)

        @block.scalar
        def _(act):
            act.wait_ge(s["setup_wc"], 1)
            nc.scalar.copy(wc[:, :].rearrange("p (a n) -> p a n", a=2), psum[:, 0:2, :]).then_inc(s["wc_ready"], 1)

            act.wait_ge(s["setup_done"], 1)

            def tok(p):
                act.wait_ge(s["tok_z"], p + 1)
                nc.scalar.activation(zt, zt, ACT.Tanh).then_inc(s["tok_tanh"], 1)
                act.wait_ge(s["tok_sub"], p + 1)
                nc.scalar.activation(sc[:, :, :], sc[:, :, :], ACT.Exp).then_inc(s["tok_exp"], 1)
                act.wait_ge(s["tok_var"], p + 1)
                nc.scalar.activation(small[0:HT, 4, 0:4], small[0:HT, 3, 0:4], ACT.Sqrt).then_inc(s["tok_sqrt"], 1)

            def blk(p, k):
                n = BLOCKS * p + k
                for j in range(STEPS):
                    act.wait_ge(s["quad_free"], n * STEPS + j + 1)
                    for g in range(2):
                        ins = nc.scalar.activation(d[:, j % RING, g, :], qp[:, :, :].rearrange("p h n -> p (h n)"),
                                                   ACT.Relu, bias=nx1t[:, bass.ds(k * BT + g * STEPS + j, 1)])
                    ins.then_inc(s["quad_act"], 1)
                act.wait_ge(s["s_ready"], n + 1)
                act.wait_ge(s["v_done"], n + 1)
                act.wait_ge(s["av_ready"], n + 1)
                for h in range(H):
                    ins = nc.scalar.activation(e[:, h, :], s_of(h), ACT.Exp, bias=bt[:, h:h + 1],
                                               accum_out=z[:, 0, h:h + 1])
                ins.then_inc(s["exps_done"], 1)
                for i in range(4):
                    act.wait_ge(s["at_filled"], 4 * n + i + 1)
                    src = (b5 if i % 2 == 0 else b6)[0:HT, :].rearrange("p (a r) -> p a r", a=4)
                    nc.scalar.copy(at[0:HT, 4 * i:4 * i + 4, :], src)\
                        .then_inc(s["bank5_read" if i % 2 == 0 else "bank6_read"], 1)

            def post(p):
                act.wait_ge(s["ot_added"], BLOCKS * (p + 1) + 1)
                nc.scalar.activation(th[:, :], ot[:, 0:NW], ACT.Tanh, scale=0.851).then_inc(s["o_tanh"], 1)
                act.wait_ge(s["post_var"], p + 1)
                nc.scalar.activation(small[0:HT, 9, 0:4], small[0:HT, 8, 0:4], ACT.Sqrt).then_inc(s["post_sqrt"], 1)
                act.wait_ge(s["x2t_ready"], p + 1)
                nc.scalar.copy(x2t[:, :], b6[:, 0:NW]).then_inc(s["x2t_done"], 1)
                act.wait_ge(s["x2t_done"], p + 1)
                act.sem_inc(s["bank6_read"], 1)

            def topk(p, t):
                q = 4 * p + t
                act.wait_ge(s["sims_ready"], q + 1)
                act.wait_ge(s["topk_done"], q + 1)
                nc.scalar.copy(sim[:, 0:512], b5[0:HT, :]).then_inc(s["bank5_read"], 1)
                nc.scalar.copy(sim[:, 512:1024], b6[0:HT, :]).then_inc(s["bank6_read"], 1)
                act.wait_ge(s["fin_sub"], q + 1)
                nc.scalar.activation(ff[:, :, :], ff[:, :, :], ACT.Exp).then_inc(s["fin_exp"], 1)

            def causal(p):
                f = [0]

                def filled():
                    f[0] += 1
                    act.wait_ge(s["c_filled"], p * CAUSAL_FILLS + f[0])

                for i in range(4):
                    filled()
                    nc.scalar.activation(qt[:, 2 * i:2 * i + 2, :].rearrange("p h n -> p (h n)"), b7[:, 0:2 * NW],
                                         ACT.Copy, scale=0.125).then_inc(s["c_read"], 1)
                for i in range(4):
                    filled()
                    nc.scalar.copy(kt[:, 2 * i:2 * i + 2, :].rearrange("p h n -> p (h n)"), b7[:, 0:2 * NW])\
                        .then_inc(s["c_read"], 1)
                for t in range(4):
                    half = t % 2
                    nj = HT * (half + 1)
                    for hp in range(4):
                        f[0] += 1
                        n = p * 16 + t * 4 + hp
                        act.wait_ge(s["c_neg"], n + 1)
                        smv = sm[:, 0:2 * nj].rearrange("p (a n) -> p a n", a=2)
                        for a in range(2):
                            ins = nc.scalar.activation(smv[:, a, :], smv[:, a, :], ACT.Exp,
                                                       bias=small[0:HT, 10, a:a + 1], accum_out=small[0:HT, 11, a:a + 1])
                        ins.then_inc(s["c_exp"], 1)
                        filled()
                        nc.scalar.copy(pt[:, 0:2 * (half + 1), :],
                                       b7[0:HT, 0:2 * nj].rearrange("p (a n) -> p a n", n=HT)).then_inc(s["c_read"], 1)
                        filled()
                        nc.scalar.copy(ott[:, hp, :], b7[:, 0:HT]).then_inc(s["c_read"], 1)
                    f[0] += 1
                assert f[0] == CAUSAL_FILLS

            with act.Fori(0, PAIRS) as p:
                tok(p)
                act.wait_ge(s["vf_done"], p + 1)
                with act.Fori(0, BLOCKS) as k:
                    blk(p, k)
                post(p)
                for t in range(4):
                    topk(p, t)
                causal(p)

        @block.tensor
        def _(pe):
            mm, tr = nc.tensor.matmul, nc.tensor.transpose
            pe.wait_ge(s["w_loaded"], 16 * len(wd))
            for g in range(4):
                ins = mm(psum[:, g // 2, 256 * (g % 2):256 * (g % 2) + 256], wpk_sb[:, g, :],
                         pkb[:, g, :, :].rearrange("p h k -> p (h k)"), start=True, stop=True)
            ins.then_inc(s["setup_wc"], 1)
            pe.wait_ge(s["setup_done"], 1)
            pe.sem_inc(s["quad_free"], RING)

            def free5(p, n):
                pe.wait_ge(s["bank5_read"], p * FILLS5 + n + 1)

            def free6(p, n):
                pe.wait_ge(s["bank6_read"], p * FILLS6 + n + 1)

            def tok(p):
                pe.wait_ge(s["x_loaded"], 80 * (p + 1))
                free5(p, FILL5_TOK)
                mm(b5[:, 0:NW], wqry2[:, :], xt[:, WIN // 2:WIN // 2 + NW], start=True, stop=True)
                free6(p, FILL6_TOK)
                mm(b6[:, 0:L], wkey2[:, :], xt[:, :], start=True, stop=True).then_inc(s["tok_proj"], 1)
                pe.wait_ge(s["tok_tanh"], p + 1)
                free5(p, FILL5_TOK + 1)
                for half in range(2):
                    for w in range(WIN):
                        o = b5[0:HT, 0:4 * WIN].rearrange("p (a b s) -> p a b s", a=2, b=2)[:, half, :, w]
                        ins = mm(o, zt[:, w * NW + half * HT:w * NW + half * HT + HT], vblk[:, :], start=True, stop=True)
                ins.then_inc(s["tok_scores"], 1)

            def prep(p):
                pe.wait_ge(s["x1_done"], p + 1)
                free6(p, FILL6_PREP)
                for half in range(2):
                    ins = tr(b6[:, half * HT:half * HT + HT],
                             x1[:, 2 * half:2 * half + 2, :].rearrange("p b c -> p (b c)"), ident[0:HT, 0:HT])
                ins.then_inc(s["x1t_ready"], 1)
                pe.wait_ge(s["prep_done"], p + 1)
                pe.wait_ge(s["exps_done"], BLOCKS * p + 1)
                for h in range(H):
                    ins = mm(s_of(h), wqh[:, h, :], x1t[:, 0:NW], start=True, stop=True)
                ins.then_inc(s["q_ready"], 1)
                pe.wait_ge(s["q_read"], p + 1)
                for half in range(2):
                    for i in range(2):
                        ins = mm(psum[0:HT, 2 * half + i, :], x1t[:, half * HT:half * HT + HT],
                                 wvf[:, 4 * i:4 * i + 4, :, :].rearrange("p h b w -> p (h b w)"), start=True, stop=True)
                ins.then_inc(s["vf_ready"], 1)

            def blk(p, k):
                n = BLOCKS * p + k
                pe.wait_ge(s["x2k_ready"], n + 1)
                x2f = x2k[:, :, :, :].rearrange("p g b j -> p (g b j)")
                pe.wait_ge(s["bank6_read"], p * FILLS6 + FILL6_BLK + 3 * k + 1)
                mm(b6[:, :], x2f, wvb[:, :], start=True, stop=True)
                pe.wait_ge(s["bank5_read"], p * FILLS5 + FILL5_BLK + 3 * k + 1)
                mm(b5[:, 0:H], x2f, wk_s[:, 1, :], start=True, stop=True).then_inc(s["v_ready"], 1)
                pe.wait_ge(s["vf_done"], p + 1)
                pe.wait_ge(s["exps_done"], n + 1)
                for h in range(H):
                    mm(s_of(h), acor[:, h, :, :, :].rearrange("p g b j -> p (g b j)"), qp[:, h, :],
                       start=(h % 2 == 0), stop=False, skip_group_check=True)
                for j in range(STEPS):
                    pe.wait_ge(s["quad_act"], n * STEPS + j + 1)
                    pe.wait_ge(s["quad_dve"], n * STEPS + j + 1)
                    for h in range(H):
                        for g in range(GR):
                            ins = mm(s_of(h, slice(32 * g, 32 * g + 32)), wpat[:, h, 15 - j:47 - j],
                                     d[:, j % RING, g, h * NW:h * NW + NW],
                                     start=False, stop=(j == STEPS - 1), skip_group_check=True)
                    ins.then_inc(s["quad_free"], 1)
                pe.wait_ge(s["quad_free"], n * STEPS + STEPS + RING)
                pe.sem_inc(s["s_ready"], 1)
                pe.wait_ge(s["attn_norm"], n + 1)
                for i in range(4):
                    bank = b5 if i % 2 == 0 else b6
                    used = 1 + i // 2
                    if i % 2 == 0:
                        pe.wait_ge(s["bank5_read"], p * FILLS5 + FILL5_BLK + 3 * k + used + 1)
                    else:
                        pe.wait_ge(s["bank6_read"], p * FILLS6 + FILL6_BLK + 3 * k + used + 1)
                    for a in range(4):
                        h, half = 2 * i + a // 2, a % 2
                        ins = tr(bank[0:HT, a * P:a * P + P], e[:, h, half * HT:half * HT + HT], ident)
                    ins.then_inc(s["at_filled"], 1)
                pe.wait_ge(s["ot_added"], n + 1)
                for h in range(H):
                    mm(b4[:, 0:NW], vbs[:, h, :, :].rearrange("p b w -> p (b w)"), e[:, h, :],
                       start=(h == 0), stop=(h == H - 1))
                pe.wait_ge(s["bank5_read"], p * FILLS5 + FILL5_BLK + 3 * k + 3 + 1)
                pe.wait_ge(s["bank6_read"], p * FILLS6 + FILL6_BLK + 3 * k + 3 + 1)
                for h in range(H):
                    for half in range(2):
                        ins = mm(b4[:, 256:384], vf[:, half, h * P:h * P + P], at[0:HT, 2 * h + half, :],
                                 start=(h == 0 and half == 0), stop=(h == H - 1 and half == 1))
                ins.then_inc(s["av_ready"], 1)

            def post(p):
                pe.wait_ge(s["og_ready"], p + 1)
                free5(p, FILL5_POST)
                for half in range(2):
                    ins = mm(b5[0:HT, half * P:half * P + P], og[:, half * HT:half * HT + HT], fan2[:, :],
                             start=True, stop=True)
                ins.then_inc(s["y_ready"], 1)
                pe.wait_ge(s["x2_done"], p + 1)
                free6(p, FILL6_POST)
                for half in range(2):
                    ins = tr(b6[:, half * HT:half * HT + HT],
                             x2[:, 2 * half:2 * half + 2, :].rearrange("p b c -> p (b c)"), ident[0:HT, 0:HT])
                ins.then_inc(s["x2t_ready"], 1)

            def topk(p, t):
                half, b = t // 2, t % 2
                r = both[b]
                pe.wait_ge(s["x2t_done"], p + 1)
                free5(p, FILL5_TOPK + t)
                mm(b5[0:HT, :], x2t[r, half * HT:half * HT + HT], wc[r, 0:512], start=True, stop=True)
                free6(p, FILL6_TOPK + t)
                mm(b6[0:HT, :], x2t[r, half * HT:half * HT + HT], wc[r, 512:1024], start=True, stop=True)\
                    .then_inc(s["sims_ready"], 1)

            def causal(p):
                f = [0]

                def free7():
                    pe.wait_ge(s["c_read"], p * CAUSAL_FILLS + f[0] + 1)
                    f[0] += 1

                for i in range(4):
                    free7()
                    for a in range(2):
                        ins = mm(b7[:, a * NW:a * NW + NW], wq2[:, 2 * i + a, :], x2t[:, :], start=True, stop=True)
                    ins.then_inc(s["c_filled"], 1)
                pe.wait_ge(s["kv_done"], (p + 1) * UNITS + 1)
                for i in range(4):
                    free7()
                    for a in range(2):
                        for half in range(2):
                            ins = tr(b7[:, a * NW + half * HT:a * NW + half * HT + HT],
                                     kv[:, half, 2 * i + a, 0, :, :].rearrange("p b c -> p (b c)"), ident[0:HT, 0:HT])
                    ins.then_inc(s["c_filled"], 1)
                for t in range(4):
                    b, half = t // 2, t % 2
                    nj = HT * (half + 1)
                    r = both[b]
                    for hp in range(4):
                        free7()
                        for a in range(2):
                            h = 2 * hp + a
                            ins = mm(b7[0:HT, a * nj:a * nj + nj], qt[r, h, half * HT:half * HT + HT], kt[r, h, 0:nj],
                                     start=True, stop=True)
                        ins.then_inc(s["c_filled"], 1)
                        pe.wait_ge(s["c_norm"], p * 16 + t * 4 + hp + 1)
                        free7()
                        for a in range(2):
                            for jh in range(half + 1):
                                c0 = (a * (half + 1) + jh) * HT
                                ins = tr(b7[0:HT, c0:c0 + HT], sm[:, c0:c0 + HT], ident[0:HT, 0:HT])
                        ins.then_inc(s["c_filled"], 1)
                        free7()
                        for a in range(2):
                            for jh in range(half + 1):
                                ins = mm(b7[64 * a:64 * a + 64, 0:HT], kv[:, jh, 2 * hp + a, 1, b, :],
                                         pt[:, a * (half + 1) + jh, :], start=(jh == 0), stop=(jh == half))
                        ins.then_inc(s["c_filled"], 1)
                    free7()
                    for hp in range(4):
                        ins = mm(b7[0:HT, 0:C], ott[:, hp, :], wo_sb[:, hp, :], start=(hp == 0), stop=(hp == 3))
                    ins.then_inc(s["c_filled"], 1)
                assert f[0] == CAUSAL_FILLS

            with pe.Fori(0, PAIRS) as p:
                tok(p)
                prep(p)
                with pe.Fori(0, BLOCKS) as k:
                    blk(p, k)
                post(p)
                for t in range(4):
                    topk(p, t)
                causal(p)

        @block.vector
        def _(dve):
            V = nc.vector
            for tile in (wkey2[:, :], wqry2[:, :], vblk[:, :], wqh[:, :, :], wvf[:, :, :, :], fan2[:, :], wq2[:, :, :],
                         pkb):
                V.memset(tile, 0.0).then_inc(s["zeroed"], 1)
            ch = Chain(dve, s["setup_dve"], SETUP_LINKS)
            ch.begin(0)
            for tile in (wpat[:, :, :], acor[:, :, :, :, :], x1t[:, :], nx1t[:, :], x2k[:, :, :, :], vbs[:, :, :, :]):
                ch.link(V.memset(tile, 0.0))
            dve.wait_ge(s["w_loaded"], 16 * len(wd))
            ch.wait()
            ch.step(V.scalar_tensor_tensor(out=wk_s[:, 0, :], in0=wkt[:, :], scalar=-1.0, in1=wkt[:, :],
                                           op0=ALU.mult, op1=ALU.max))
            ch.step(V.tensor_scalar(wk_s[:, 0, :], wk_s[:, 0, :], TINY, None, ALU.max))
            ch.link(V.tensor_scalar(wk_s[:, 1, :], wk_s[:, 0, :], -0.125, None, ALU.mult))
            ch.link(V.tensor_scalar(wk_s[:, 2, :], wk_s[:, 0, :], 0.125, None, ALU.mult))
            ch.step(V.tensor_scalar(wk_s[:, 3, :], wkt[:, :], 0.0, 2.0, ALU.is_ge, ALU.mult))
            ch.step(V.tensor_scalar(wk_s[:, 3, :], wk_s[:, 3, :], -1.0, None, ALU.add))
            ch.step(V.tensor_tensor(wk_s[:, 3, :], wk_s[:, 3, :], wk_s[:, 0, :], ALU.mult))
            ch.step(V.reciprocal(wk_s[:, 4, :], wk_s[:, 3, :]))
            for b, r in enumerate(both):
                c0 = 15 + 16 * b
                ch.link(V.tensor_scalar(wpat[r, :, c0:c0 + 1], wk_s[r, 0, :].unsqueeze(2), -0.25, None, ALU.mult))
                for g in range(GR):
                    ch.link(V.tensor_copy(acor[r, :, g, b, :], wk_s[r, 2, :].unsqueeze(2).to_broadcast([C, H, STEPS])))
            ch.step(V.tensor_scalar(fan2[:, :], fan2[:, :], 0.5, None, ALU.mult))
            ch.end()
            dve.wait_ge(s["wc_ready"], 1)
            for n in CREDITED:
                dve.sem_inc(s[n], 1)
            dve.sem_inc(s["slot_free"], SLOTS)
            dve.sem_inc(s["setup_done"], 1)

            def var_of(src, row, cn):
                a, b = small[0:HT, row, 0:4], small[0:HT, row + 1, 0:4]
                cn.step(V.tensor_reduce(a, src, AX.X, ALU.add))
                cn.step(V.tensor_scalar(a, a, 1.0 / C, None, ALU.mult))
                cn.step(V.tensor_tensor(cen[:, :, :], src, a.unsqueeze(2).to_broadcast([HT, 4, C]), ALU.subtract))
                cn.step(V.tensor_tensor(sq[:, :, :], cen[:, :, :], cen[:, :, :], ALU.mult))
                cn.step(V.tensor_reduce(b, sq[:, :, :], AX.X, ALU.add))

            tokc = Chain(dve, s["tok_dve"], TOK_LINKS)

            def tok(p):
                cn = tokc
                cn.begin(p)
                dve.wait_ge(s["tok_proj"], p + 1)
                V.tensor_scalar(qry[:, :], b5[:, 0:NW], tokb[:, 0:1], None, ALU.add).then_inc(s["bank5_read"], 1)
                V.tensor_copy(key[:, :], b6[:, 0:L]).then_inc(s["bank6_read"], 1)
                dve.wait_ge(s["bank5_read"], p * FILLS5 + FILL5_TOK + 2)
                dve.wait_ge(s["bank6_read"], p * FILLS6 + FILL6_TOK + 2)
                win = bass.AP(key[:, :].tensor, 0, [[L, P], [1, WIN], [1, NW]])
                V.tensor_tensor(zt.rearrange("p (s w) -> p s w", s=WIN), win,
                                qry[:, :].unsqueeze(1).to_broadcast([P, WIN, NW]), ALU.add).then_inc(s["tok_z"], 1)
                dve.wait_ge(s["tok_scores"], p + 1)
                scp = b5[0:HT, 0:4 * WIN].rearrange("p (a s) -> p a s", a=4)
                m = small[0:HT, 0, 0:4]
                cn.step(V.tensor_reduce(m, scp, AX.X, ALU.max))
                V.tensor_tensor(sc[:, :, :], scp, m.unsqueeze(2).to_broadcast([HT, 4, WIN]), ALU.subtract)\
                    .then_inc(s["tok_sub"], 1)
                dve.wait_ge(s["tok_exp"], p + 1)
                dve.sem_inc(s["bank5_read"], 1)
                cn.step(V.tensor_reduce(small[0:HT, 1, 0:4], sc[:, :, :], AX.X, ALU.add))
                cn.step(V.reciprocal(small[0:HT, 1, 0:4], small[0:HT, 1, 0:4]))
                cn.step(V.tensor_tensor(sc[:, :, :], sc[:, :, :],
                                        small[0:HT, 1, 0:4].unsqueeze(2).to_broadcast([HT, 4, WIN]), ALU.mult))
                dve.wait_ge(s["x_loaded"], 80 * (p + 1))
                x3 = xw.rearrange("p (a c) -> p a c", c=C)
                cn.step(V.tensor_tensor(x3, x3, sc[:, :, :].rearrange("p a s -> p (a s)").unsqueeze(2)
                                        .to_broadcast([HT, 4 * WIN, C]), ALU.mult))
                V.tensor_reduce(h1[:, :, :], xw.rearrange("p (a s c) -> p a c s", a=4, s=WIN), AX.X, ALU.add)\
                    .then_inc(s["tok_done"], 1)
                dve.wait_ge(s["tok_done"], p + 2)
                var_of(h1[:, :, :], 2, cn)
                V.tensor_scalar(small[0:HT, 3, 0:4], small[0:HT, 3, 0:4], 1.0 / C, EPS, ALU.mult, ALU.add)\
                    .then_inc(s["tok_var"], 1)
                dve.wait_ge(s["tok_sqrt"], p + 1)
                r = small[0:HT, 5, 0:4]
                cn.step(V.reciprocal(r, small[0:HT, 4, 0:4]))
                V.tensor_tensor(x1[:, :, :], cen[:, :, :], r.unsqueeze(2).to_broadcast([HT, 4, C]), ALU.mult)\
                    .then_inc(s["x1_done"], 1)
                dve.wait_ge(s["x1_done"], p + 1)
                cn.step(V.tensor_tensor(hx[:, :, :], h1[:, :, :], x1[:, :, :], ALU.add))
                cn.step(V.tensor_tensor(hx[:, :, :], hx[:, :, :], fb[0:HT, :].unsqueeze(1).to_broadcast([HT, 4, C]),
                                        ALU.add))
                cn.end()

            prepc = Chain(dve, s["prep_dve"], PREP_LINKS)

            def prep(p):
                cn = prepc
                cn.begin(p)
                dve.wait_ge(s["x1t_ready"], p + 1)
                cn.link(V.tensor_copy(x1t[:, 0:NW], b6[:, 0:NW]))
                cn.link(V.tensor_scalar(nx1t[:, 0:NW], b6[:, 0:NW], -1.0, None, ALU.mult))
                cn.wait()
                dve.sem_inc(s["bank6_read"], 1)
                dve.sem_inc(s["prep_done"], 1)
                cn.link(V.memset(ot[:, :], 0.0))
                dve.wait_ge(s["q_ready"], p + 1)
                for h in range(H):
                    cn.link(V.tensor_scalar(qp[:, h, :], s_of(h), bq[:, h:h + 1], wk_s[:, 4, h:h + 1],
                                            ALU.add, ALU.mult))
                cn.wait()
                dve.sem_inc(s["q_read"], 1)
                dve.wait_ge(s["vf_ready"], p + 1)
                for half in range(2):
                    for i in range(2):
                        hs = slice(4 * i * C, 4 * (i + 1) * C)
                        ins = V.tensor_tensor(
                            vf[:, half, i * 512:(i + 1) * 512].rearrange("p (h b w) -> p h b w", h=4, b=2),
                            psum[0:HT, 2 * half + i, :].rearrange("p (h b w) -> p h b w", h=4, b=2),
                            bvf[0:HT, hs].rearrange("p (h w) -> p h w", h=4).unsqueeze(2).to_broadcast([HT, 4, 2, C]),
                            ALU.add)
                        if half and i:
                            ins.then_inc(s["vf_done"], 1)
                        else:
                            cn.link(ins)
                cn.end()

            blkc = Chain(dve, s["blk_dve"], BLK_LINKS)

            def blk(p, k):
                n = BLOCKS * p + k
                cn = blkc
                cn.begin(n)
                dve.wait_ge(s["v_ready"], n + 1)
                for b, r in enumerate(both):
                    ins = V.tensor_copy(x2k[r, :, b, :],
                                        x1t[r, bass.ds(k * BT, BT)].rearrange("p (g j) -> p g j", g=GR))
                    if b == 0:
                        cn.step(ins)
                ins.then_inc(s["x2k_ready"], 1)
                dve.wait_ge(s["v_ready"], n + 2)
                dve.wait_ge(s["exps_done"], n + 1)
                dve.wait_ge(s["av_ready"], n + 1)
                V.tensor_copy(bt[:, :], b5[:, 0:H]).then_inc(s["bank5_read"], 1)
                V.tensor_tensor(v1, b6[:, :].rearrange("p (h w) -> p h w", h=H),
                                bvb[:, :].rearrange("p (h w) -> p h w", h=H), ALU.add).then_inc(s["bank6_read"], 1)
                dve.wait_ge(s["bank6_read"], p * FILLS6 + FILL6_BLK + 3 * k + 2)
                for b in range(2):
                    ins = V.tensor_scalar(vbs[:, :, b, :], v1, con[:, bass.ds(C_ROWS + 2 * k + b, 1)], None, ALU.mult)
                    if b == 0:
                        cn.link(ins)
                ins.then_inc(s["v_done"], 1)
                for j in range(STEPS):
                    dve.wait_ge(s["quad_free"], n * STEPS + j + 1)
                    for g in range(2, GR):
                        ins = V.tensor_scalar(d[:, j % RING, g, :], qp[:, :, :].rearrange("p h n -> p (h n)"),
                                              x1t[:, bass.ds(k * BT + g * STEPS + j, 1)], 0.0, ALU.subtract, ALU.max)
                    ins.then_inc(s["quad_dve"], 1)
                dve.wait_ge(s["exps_done"], n + 2)
                cn.step(V.tensor_scalar(z[:, 1, :], z[:, 0, :], 1.0, None, ALU.add))
                cn.step(V.reciprocal(z[:, 2, :], z[:, 1, :]))
                for h in range(H):
                    ins = V.tensor_scalar(e[:, h, :], e[:, h, :], z[:, 2, h:h + 1], None, ALU.mult)
                    if h < H - 1:
                        cn.link(ins)
                ins.then_inc(s["attn_norm"], 1)
                dve.wait_ge(s["av_ready"], n + 2)
                cn.step(V.tensor_tensor(ot[:, 0:NW], ot[:, 0:NW], b4[:, 0:NW], ALU.add))
                for b, r in enumerate(both):
                    o = ot[r, bass.ds(k * BT, BT)].rearrange("p (g j) -> p g j", g=GR)
                    ins = V.tensor_tensor(o, o, b4[r, 256:384].rearrange("p (g b j) -> p g b j", g=GR, b=2)[:, :, b, :],
                                          ALU.add)
                    if b == 0:
                        cn.step(ins)
                ins.then_inc(s["ot_added"], 1)
                cn.end()

            postc = Chain(dve, s["post_dve"], POST_LINKS)

            def post(p):
                cn = postc
                cn.begin(p)
                dve.wait_ge(s["o_tanh"], p + 1)
                V.scalar_tensor_tensor(out=og[:, :], in0=th[:, :], scalar=1.0, in1=ot[:, 0:NW],
                                       op0=ALU.add, op1=ALU.mult).then_inc(s["og_ready"], 1)
                dve.wait_ge(s["y_ready"], p + 1)
                cn.step(V.tensor_tensor(h2[:, :, :], b5[0:HT, 0:2 * P].rearrange("p (a c) -> p a c", a=4),
                                        hx[:, :, :], ALU.add))
                dve.sem_inc(s["bank5_read"], 1)
                var_of(h2[:, :, :], 7, cn)
                V.tensor_scalar(small[0:HT, 8, 0:4], small[0:HT, 8, 0:4], 1.0 / C, EPS, ALU.mult, ALU.add)\
                    .then_inc(s["post_var"], 1)
                dve.wait_ge(s["post_sqrt"], p + 1)
                r = small[0:HT, 7, 0:4]
                cn.step(V.reciprocal(r, small[0:HT, 9, 0:4]))
                cn.step(V.tensor_tensor(x2[:, :, :], cen[:, :, :], r.unsqueeze(2).to_broadcast([HT, 4, C]), ALU.mult))
                dve.sem_inc(s["x2_done"], 1)
                cn.end()

            topc = Chain(dve, s["topk_dve"], TOPK_LINKS, s["dve_passed"])

            def topk(p, t):
                q = 4 * p + t
                half, b = t // 2, t % 2
                cn = topc
                cn.begin(q)
                dve.wait_ge(s["bank5_read"], p * FILLS5 + FILL5_TOPK + t + 2)
                dve.wait_ge(s["bank6_read"], p * FILLS6 + FILL6_TOPK + t + 2)
                dve.sem_inc(s["dve_passed"], 1)
                lists = [(sim[:, 64 * i:64 * i + 64], tv[:, i // H, i % H, :], ti[:, i // H, i % H, :])
                         for i in range(2 * H)]

                def top16(lists):
                    for src, val, pos in lists:
                        cn.link(V.max(val[:, 0:8], src))
                    cn.hold()
                    for src, val, pos in lists:
                        cn.link(V.max_index(pos[:, 0:8], val[:, 0:8], src))
                    cn.hold()
                    for src, val, pos in lists:
                        cn.link(V.match_replace(src, val[:, 0:8], src, LOWEST))
                    cn.hold()
                    for src, val, pos in lists:
                        cn.link(V.max(val[:, 8:16], src))
                    cn.hold()
                    for src, val, pos in lists:
                        cn.link(V.max_index(pos[:, 8:16], val[:, 8:16], src))
                    cn.hold()

                top16(lists)
                cn.link(V.tensor_copy(code[:, 0, :, :], ti[:, 0, :, :]))
                hoff = con[0:HT, C_HOFF:C_END].rearrange("p (h m) -> p h m", h=H)
                cn.step(V.scalar_tensor_tensor(out=code[:, 1, :, :], in0=ti[:, 1, :, :], scalar=float(NK),
                                               in1=hoff, op0=ALU.mult, op1=ALU.add))
                for dst, src in ((cs, tv), (cc, code)):
                    o = 0
                    for i0, ni, nj in TIES:
                        cn.link(V.tensor_tensor(
                            dst[:, :, o:o + ni * nj].rearrange("p h (i j) -> p h i j", i=ni),
                            src[:, 0, :, i0:i0 + ni].unsqueeze(3).to_broadcast([HT, H, ni, nj]),
                            src[:, 1, :, 0:nj].unsqueeze(2).to_broadcast([HT, H, ni, nj]), ALU.add))
                        o += ni * nj
                cn.hold()
                top16([(cs[:, h, :], fv[:, h, :], fi[:, h, :]) for h in range(H)])
                V.tensor_tensor(ff[:, :, :], fv[:, :, :], fv[:, :, 0:1].to_broadcast([HT, H, TOP]), ALU.subtract)\
                    .then_inc(s["fin_sub"], 1)
                cn.step(V.tensor_copy(keyf[:, :, :], fi[:, :, :]))
                iota = con[0:HT, C_IOTA:C_IOTA + CAND]
                for hg in range(2):
                    kf = keyf[:, 4 * hg:4 * hg + 4, :].rearrange("p h m -> p (h m)")
                    eq3 = eq.rearrange("p (a c) -> p a c", c=CAND)
                    cn.step(V.tensor_tensor(eq3, kf.unsqueeze(2).to_broadcast([HT, 4 * TOP, CAND]),
                                            iota.unsqueeze(1).to_broadcast([HT, 4 * TOP, CAND]), ALU.is_equal))
                    eq4 = eq.rearrange("p (h m c) -> p h m c", h=4, c=CAND)
                    cn.step(V.tensor_tensor(eq4, eq4, cc[:, 4 * hg:4 * hg + 4, :].unsqueeze(2)
                                            .to_broadcast([HT, 4, TOP, CAND]), ALU.mult))
                    cn.step(V.tensor_reduce(kf, eq3, AX.X, ALU.add))
                V.tensor_copy(idx[:, half, :, b, :], keyf[:, :, :]).then_inc(s["idx_ready"], 1)
                dve.wait_ge(s["fin_exp"], q + 1)
                zz = small[0:HT, 6, 0:H]
                cn.step(V.tensor_reduce(zz, ff[:, :, :], AX.X, ALU.add))
                cn.step(V.reciprocal(zz, zz))
                cn.step(V.tensor_tensor(wt[:, half, :, b, :], ff[:, :, :], zz.unsqueeze(2).to_broadcast([HT, H, TOP]),
                                        ALU.mult))
                dve.sem_inc(s["topk_done"], 1)
                cn.end()

            sumc = Chain(dve, s["sum_dve"], SUM_LINKS)

            def weigh(p, u):
                half, h, b = u // (2 * H), u // 2 % H, u % 2
                cn = sumc
                cn.begin(p * UNITS + u)
                dve.wait_ge(loaded[u % SLOTS], (p * (UNITS // SLOTS) + u // SLOTS + 1) * 16 * TOP)
                g = g_rows[:, u % SLOTS, :, :]
                cn.step(V.tensor_tensor(g, g, wt[:, half, h, b, :].unsqueeze(2).to_broadcast([HT, TOP, 2 * C]), ALU.mult))
                V.tensor_reduce(kv[:, half, h, :, b, :], g.rearrange("p m (a c) -> p a c m", a=2), AX.X, ALU.add)\
                    .then_inc(s["kv_done"], 1)
                dve.wait_ge(s["kv_done"], p * UNITS + u + 2)
                dve.sem_inc(s["slot_free"], 1)

            cauc = Chain(dve, s["c_dve"], CAUSAL_LINKS)

            def causal(p):
                cn = cauc
                cn.begin(p)
                f = [8]
                mask = con[0:HT, C_MASK:C_MASK + NW]
                for t in range(4):
                    b, half = t // 2, t % 2
                    nj = HT * (half + 1)
                    for hp in range(4):
                        n = p * 16 + t * 4 + hp
                        f[0] += 1
                        dve.wait_ge(s["c_filled"], p * CAUSAL_FILLS + f[0])
                        smv = sm[:, 0:2 * nj].rearrange("p (a n) -> p a n", a=2)
                        cn.step(V.tensor_tensor(smv, b7[0:HT, 0:2 * nj].rearrange("p (a n) -> p a n", a=2),
                                                mask[:, NW - nj:NW].unsqueeze(1).to_broadcast([HT, 2, nj]), ALU.add))
                        dve.sem_inc(s["c_read"], 1)
                        V.tensor_reduce(small[0:HT, 10, 0:2], smv, AX.X, ALU.max, negate=True).then_inc(s["c_neg"], 1)
                        dve.wait_ge(s["c_exp"], n + 1)
                        cn.step(V.reciprocal(small[0:HT, 10, 2:4], small[0:HT, 11, 0:2]))
                        cn.link(V.tensor_scalar(smv[:, 0, :], smv[:, 0, :], small[0:HT, 10, 2:3], None, ALU.mult))
                        cn.step(V.tensor_scalar(smv[:, 1, :], smv[:, 1, :], small[0:HT, 10, 3:4], None, ALU.mult))
                        dve.sem_inc(s["c_norm"], 1)
                        f[0] += 2
                    f[0] += 1
                    dve.wait_ge(s["c_filled"], p * CAUSAL_FILLS + f[0])
                    hb = 2 * half + b
                    if t == 0:
                        dve.wait_ge(s["stored"], 64 * p + 1)
                    V.tensor_tensor(outb[:, t, :], b7[0:HT, 0:C], h2[:, hb, :], ALU.add).then_inc(s["c_read"], 1)
                    dve.wait_ge(s["c_read"], p * CAUSAL_FILLS + f[0] + 1)
                    dve.sem_inc(s["c_out"], 1)
                cn.end()

            with dve.Fori(0, PAIRS) as p:
                tok(p)
                prep(p)
                with dve.Fori(0, BLOCKS) as k:
                    blk(p, k)
                post(p)
                for t in range(4):
                    topk(p, t)
                for u in range(UNITS):
                    weigh(p, u)
                causal(p)


def kernel(x, L0_tok_W_qry, L0_tok_W_key, L0_tok_v, L0_tok_b, L0_attn_wqv_w, L0_attn_wqv_b, L0_attn_wk,
           L0_attn_fanin_w, L0_attn_fanin_b, L0_ffn_Wq_pk, L0_ffn_pk_keys, L0_ffn_Wq, L0_ffn_keys_table,
           L0_ffn_values_table, L0_ffn_Wo):
    import concourse.bacc as bacc
    from concourse.bass_utils import run_bass_kernel_spmd

    def a(t):
        return np.asarray(t)

    x = a(x)
    bias = a(L0_attn_wqv_b)
    arrays = {
        "x": x,
        "xT": x.transpose(0, 2, 1).reshape(PAIRS, 2 * C, L),
        "w_qry": a(L0_tok_W_qry), "w_key": a(L0_tok_W_key), "v_tok": a(L0_tok_v), "b_tok": a(L0_tok_b),
        "wqvT": a(L0_attn_wqv_w).T, "bqT": bias[:H * C].reshape(H, C).T, "b_qv": bias,
        "wkT": a(L0_attn_wk).T, "faninT": a(L0_attn_fanin_w).T, "b_fanin": a(L0_attn_fanin_b),
        "wpkT": a(L0_ffn_Wq_pk).T.reshape(4, P, C),
        "pkT": a(L0_ffn_pk_keys).transpose(0, 2, 3, 1).reshape(4, P, NK),
        "wq": a(L0_ffn_Wq),
        "tables": np.concatenate([a(L0_ffn_keys_table), a(L0_ffn_values_table)], axis=1),
        "wo": a(L0_ffn_Wo),
        "consts": constants(),
    }
    nc = bacc.Bacc("TRN2", target_bir_lowering=False, num_devices=1)
    ins, aps = {}, []
    for name, v in arrays.items():
        v = np.ascontiguousarray(v)
        ins[f"in_{name}"] = v
        aps.append(nc.dram_tensor(f"in_{name}", v.shape, mybir.dt.from_np(v.dtype), kind="ExternalInput").ap())
    out = nc.dram_tensor("out_h", (NB, NW, C), F32, kind="ExternalOutput").ap()
    build(nc, *aps, out)
    r = run_bass_kernel_spmd(nc, [ins], core_ids=[0])
    return r.results[0]["out_h"]
```

```python
from contextlib import ExitStack

import numpy as np

import concourse.bass as bass
from concourse import mybir

F32 = mybir.dt.float32
U32 = mybir.dt.uint32
ALU = mybir.AluOpType
ACT = mybir.ActivationFunctionType
AX = mybir.AxisListType

P = 128
NB, L, C = 16, 256, 64
WIN = 9
NW = L - WIN + 1
PAIRS = NB // 2
HT = NW // 2
H = 8
GR = 4
STEPS = 16
BT = GR * STEPS
BLOCKS = 4
RING = 2
NK = 64
TOP = 16
TIES = [(0, 1, 16), (1, 1, 8), (2, 3, 5), (5, 3, 2), (8, 8, 1)]
CAND = sum(n * m for _, n, m in TIES)
EPS = 1e-5
TINY = 1e-20
SLOTS = 2
UNITS = 4 * H
EARLY = 2
UNIT_AT, UNIT_AT_LAST = (0, 3, 6, 9, 12, 15), (0, 2, 4, 6, 8, 10, 12, 14)
PER_BLOCK = len(UNIT_AT)
LATE = UNITS - EARLY - (BLOCKS - 1) * PER_BLOCK - len(UNIT_AT_LAST)
ACT_QUAD = (3, 2)
VB_FILL = 2
KEYS_AT = {j: 2 if j in (3, 5, 7) else 1 for j in range(1, STEPS)}
KEYS_EXP = 12
LOWEST = -3.0e38
MASKED = -1.0e30

C_ID = 0
C_MASK = P
C_ROWS = C_MASK + 4 * NW
C_BATCH = C_ROWS + 2 * BLOCKS
C_IOTA = C_BATCH + 4
C_HOFF = C_IOTA + CAND
C_END = C_HOFF + H * TOP


def constants():
    c = np.zeros((P, C_END), np.float32)
    c[:, C_ID:C_ID + P] = np.eye(P)
    i, j = np.arange(HT)[:, None], np.arange(HT)[None, :]
    for t in range(4):
        m = c[:HT, C_MASK + t * NW:C_MASK + (t + 1) * NW]
        m[:, t // 2 * HT:t // 2 * HT + HT] = np.where(j <= i, 0.0, MASKED)
        if t < 2:
            m[:, HT:] = MASKED
    r = np.arange(P)
    g, b, s = r // 32, r // 16 % 2, r % 16
    for k in range(BLOCKS):
        t = k * BT + g * STEPS + s
        for bb in range(2):
            c[:, C_ROWS + 2 * k + bb] = (b == bb) & (t < NW)
    for t in range(4):
        c[:, C_BATCH + t] = r // C == t % 2
    c[:, C_IOTA:C_IOTA + CAND] = np.arange(CAND)
    c[:, C_HOFF:C_END] = np.repeat(np.arange(H) * NK * NK, TOP)
    return c


class Chain:

    def __init__(self, eng, sem, per, passed=None):
        self.eng, self.sem, self.per, self.passed = eng, sem, per, passed

    def begin(self, instance):
        self.base, self.n = instance * self.per, 0

    def link(self, ins):
        self.n += 1
        ins.then_inc(self.sem, 1)

    def wait(self):
        self.eng.wait_ge(self.sem, self.base + self.n)

    def hold(self):
        self.wait()
        self.eng.sem_inc(self.passed, 1)

    def step(self, ins):
        self.link(ins)
        self.wait()

    def end(self):
        assert self.n == self.per, (self.sem, self.n)


TOK_LINKS, PREP_LINKS, BLK_LINKS, POST_LINKS, TOPK_LINKS, SUM_LINKS, TILE_LINKS, TURN_LINKS = 15, 14, 15, 10, 148, 1, 16, 6
SETUP_LINKS = 19

FILLS = 4 * 4 + 1
CREDITED = ("tok_done", "exps_done", "av_ready", "topk_done", "sims_ready", "v_ready", "ot_added", "at_read",
            "sims_read", "c_read", "kt_read", "stored")


def build(nc, x, xT, w_qry, w_key, v_tok, b_tok, wqvT, bqT, b_qv, wkT, faninT, b_fanin,
          wpkT, pkT, wq, tables, wo, consts, out):
    with ExitStack() as ctx:
        def sb(name, shape, dt=F32):
            return ctx.enter_context(nc.sbuf_tensor(name, shape, dt))

        def sem(name):
            return ctx.enter_context(nc.semaphore(name))

        psum = ctx.enter_context(nc.psum_tensor("psum", [P, 8, 512], F32))

        con = sb("con", [P, C_END])
        wkey2, wqry2 = sb("wkey2", [P, P]), sb("wqry2", [P, P])
        tokb = sb("tokb", [P, 1])
        vblk = sb("vblk", [P, 2])
        wqh = sb("wqh", [P, H, P])
        bq = sb("bq", [P, H])
        wkt = sb("wkt", [P, H])
        wk_s = sb("wk_s", [P, 5, H])
        wvf = sb("wvf", [P, H, 2, C])
        wvb = sb("wvb", [P, H * C])
        bvf, bvb = sb("bvf", [P, H * C]), sb("bvb", [P, H * C])
        fb = sb("fb", [P, C])
        fan2 = sb("fan2", [P, P])
        wq2 = sb("wq2", [P, H, P])
        wo2 = sb("wo2", [P, H, C])
        wc = sb("wc", [P, 2 * H * NK])
        wpat = sb("wpat", [P, H, 47])
        acor = sb("acor", [P, H, 2, STEPS])

        sc = sb("sc", [HT, 4, WIN])
        small = sb("small", [P, 12, 8])
        hx = sb("hx", [HT, 4, C])
        h2, h2p = sb("h2", [HT, 4, C]), sb("h2p", [HT, 4, C])
        xm, xmp = sb("xm", [P, 4, HT]), sb("xmp", [P, 4, HT])
        x1t, nx1t = sb("x1t", [P, BLOCKS * BT]), sb("nx1t", [P, BLOCKS * BT])
        qp = sb("qp", [P, H, NW])
        vf = sb("vf", [HT, 2, H * P])
        x2k = sb("x2k", [P, GR, 2, STEPS])
        bt = sb("bt", [P, H])
        vbs = sb("vbs", [P, H, 2, C])
        z = sb("z", [P, 3, H])
        ot = sb("ot", [P, BLOCKS * BT])
        xk = sb("xk", [P, HT])
        tv, ti = sb("tv", [HT, 2, H, TOP]), sb("ti", [HT, 2, H, TOP], U32)
        code = sb("code", [HT, 2, H, TOP])
        fv, fi = tv[:, 0, :, :], ti[:, 0, :, :]
        ff, keyf = code[:, 0, :, :], code[:, 1, :, :]
        idx = sb("idx", [HT, 4, H * TOP], U32)
        wt = sb("wt", [HT, 4 * H * TOP])
        g_rows = sb("g_rows", [HT, SLOTS, TOP, 2 * C])
        kv = sb("kv", [HT, 4 * H * 2 * C])
        vv = sb("vv", [HT, 2, H, 2, C])
        kt = sb("kt", [P, H, NW])
        qk = sb("qk", [P, 2, HT])
        sm = sb("sm", [HT, 2, NW])
        pt = sb("pt", [HT, 4, HT])
        ott = sb("ott", [P, H, HT])
        outb = sb("outb", [HT, 4, C])
        e_keys = sb("e_keys", [P, H * NW])
        e = e_keys[:, :].rearrange("p (h n) -> p h n", h=H)
        sim = e_keys[0:HT, 0:2 * H * NK]
        cs = e_keys[0:HT, 1024:1024 + H * CAND].rearrange("p (h c) -> p h c", h=H)
        cc = e_keys[0:HT, 1024 + H * CAND:1024 + 2 * H * CAND].rearrange("p (h c) -> p h c", h=H)
        at_eq = sb("at_eq", [P, 2 * H * P])
        at = at_eq[:, :].rearrange("p (a n) -> p a n", n=P)
        v1 = at_eq[:, 0:H * C].rearrange("p (h w) -> p h w", w=C)
        eq = at_eq[0:HT, 0:2 * TOP * CAND]

        ring = sb("ring", [P, RING * GR * H * NW])
        d = ring[:, :].rearrange("p (q g n) -> p q g n", q=RING, g=GR)
        at_ = [0]

        def part(n, rows=P):
            a = ring[0:rows, at_[0]:at_[0] + n]
            at_[0] += n
            return a
        xt = part(L)
        qry = part(NW)
        key_at = at_[0]
        key = part(L)
        zt = part(WIN * NW)
        xw = part(4 * WIN * C, HT)
        h1, x1, x2, cen, sq = (part(4 * C, HT).rearrange("p (a c) -> p a c", c=C) for _ in range(5))
        og, th = part(NW), part(NW)
        kc = part(2 * H * P, HT).rearrange("p (f h b c) -> p f h b c", f=2, h=H, b=2)
        assert at_[0] <= RING * GR * H * NW
        wpk_sb = ring[:, 0:4 * P].rearrange("p (g c) -> p g c", g=4)
        pkb = ring[:, 4 * P:4 * P + 4 * 4 * NK].rearrange("p (g h k) -> p g h k", g=4, h=4)

        ident = con[:, C_ID:C_ID + P]
        S = psum[:, 0:4, 0:2 * NW].rearrange("p k (h n) -> p k h n", h=2)

        def s_of(h, rows=slice(0, P)):
            return S[rows, h // 2, h % 2, :]

        b4, b5, b6, b7 = (psum[:, k, :] for k in (4, 5, 6, 7))

        names = """zeroed w_loaded setup_dve setup_wc wc_ready setup_done
            x_loaded tok_proj tok_z tok_tanh tok_scores tok_sub tok_exp tok_var tok_sqrt tok_dve tok_done x1_done
            x1t_ready prep_done q_ready q_read vf_ready vf_done prep_dve
            x2k_ready v_ready v_done quad_act quad_dve quad_free s_ready exps_done attn_norm at_filled at_read
            av_ready ot_added blk_dve
            o_tanh og_ready y_ready post_var post_sqrt x2_done x2t_ready xm_ready post_dve
            xk_ready sims_ready sims_read topk_done fin_sub fin_exp idx_ready topk_dve
            dve_passed act_passed pool_passed sp_passed
            slot_free sum_dve
            kc_ready kt_filled kt_read turn_dve
            c_filled c_read c_exp c_neg c_norm c_out c_dve stored""".split()
        s = {n: sem(n) for n in names}
        loaded = [sem(f"slot{i}_loaded") for i in range(SLOTS)]

        ZEROS = 8
        both = [slice(0, C), slice(C, 2 * C)]
        wd = [(con[:, :], consts)]
        for b, r in enumerate(both):
            wd += [(wkey2[r, r], w_key), (wqry2[r, r], w_qry), (tokb[r, :], b_tok.unsqueeze(1)),
                   (vblk[r, b:b + 1], v_tok.unsqueeze(1)),
                   (wqh[r, :, r], wqvT[:, 0:512].rearrange("c (h w) -> c h w", h=H)),
                   (bq[r, :], bqT), (wkt[r, :], wkT),
                   (wvf[r, :, b, :], wqvT[:, 512:1024].rearrange("c (h w) -> c h w", h=H)),
                   (wvb[r, :], wqvT[:, 1024:1536]), (fan2[r, r], faninT),
                   (wq2[r, :, r], wq.rearrange("c (h w) -> c h w", h=H)),
                   (wpk_sb[:, :, r], wpkT.rearrange("g p c -> p g c"))]
        wd += [(bvf[:, :], b_qv[512:1024].partition_broadcast(P)),
               (bvb[:, :], b_qv[1024:1536].partition_broadcast(P)),
               (fb[:, :], b_fanin.partition_broadcast(P))]
        wd += [(wo2[r, :, :], wo.rearrange("(h w) n -> w h n", h=H)) for r in both]
        wd += [(pkb[32 * a:32 * a + 32, :, a, :], pkT[:, 32 * a:32 * a + 32, :].rearrange("g p k -> p g k"))
               for a in range(4)]

        block = ctx.enter_context(nc.Block())

        def run(eng, iteration):
            iteration(0, now=True, back1=False, back2=False)
            iteration(1, now=True, back1=True, back2=False)
            with eng.Fori(2, PAIRS) as p:
                iteration(p, now=True, back1=True, back2=True)
            iteration(PAIRS, now=False, back1=True, back2=True)
            iteration(PAIRS + 1, now=False, back1=False, back2=True)

        def run_blocks(eng, p, blk, now, back1, back2):
            with eng.Fori(0, BLOCKS - 1) as k:
                blk(p, k, now, back1, back1, back2)
            blk(p, BLOCKS - 1, now, False, back1, back2)

        @block.sync
        def _(sp):
            sp.wait_ge(s["zeroed"], ZEROS)
            for dst, src in wd:
                sp.dma_start(dst, src).then_inc(s["w_loaded"], 16)
            sp.wait_ge(s["setup_done"], 1)

            def iteration(p, now, back1, back2):
                if now:
                    sp.wait_ge(s["tok_done"], p + 1)
                    sp.wait_ge(s["exps_done"], BLOCKS * p + 1)
                    sp.sem_inc(s["sp_passed"], 1)
                    sp.dma_start(xt, xT[bass.ds(p, 1), :, :].rearrange("a p l -> p (a l)"))\
                        .then_inc(s["x_loaded"], 16)
                    for hb in range(4):
                        half, b = hb // 2, hb % 2
                        src = bass.AP(x.tensor, p * (2 * L * C) + (b * L + half * HT) * C, [[C, HT], [1, WIN * C]])
                        sp.dma_start(xw[:, hb * WIN * C:(hb + 1) * WIN * C], src).then_inc(s["x_loaded"], 16)
                if back2:
                    for t in range(4):
                        sp.wait_ge(s["c_out"], 4 * (p - 2) + t + 1)
                        sp.sem_inc(s["sp_passed"], 1)
                        half, b = t // 2, t % 2
                        sp.dma_start(out[bass.ds(2 * (p - 2) + b, 1), half * HT:(half + 1) * HT, :]
                                     .rearrange("a t c -> (a t) c"), outb[:, t, :]).then_inc(s["stored"], 16)

            run(sp, iteration)
            sp.wait_ge(s["stored"], 16 * 4 * PAIRS + 1)

        @block.gpsimd
        def _(pool):
            pool.wait_ge(s["setup_done"], 1)
            with pool.Fori(0, PAIRS) as p:
                for u in range(UNITS):
                    t, h = u // H, u % H
                    if h == 0:
                        pool.wait_ge(s["idx_ready"], 4 * p + t + 1)
                    pool.wait_ge(s["slot_free"], p * UNITS + u + 1)
                    pool.sem_inc(s["pool_passed"], 1)
                    for m in range(TOP):
                        nc.gpsimd.indirect_dma_start(
                            g_rows[:, u % SLOTS, m, :], None, tables,
                            bass.IndirectOffsetOnAxis(idx[:, t, h * TOP + m:h * TOP + m + 1], 0))\
                            .then_inc(loaded[u % SLOTS], 16)

        @block.scalar
        def _(act):
            act.wait_ge(s["setup_wc"], 1)
            nc.scalar.copy(wc[:, :].rearrange("p (a n) -> p a n", a=2), psum[:, 0:2, :]).then_inc(s["wc_ready"], 1)

            act.wait_ge(s["setup_done"], 1)

            def tok(p):
                act.wait_ge(s["tok_z"], p + 1)
                nc.scalar.activation(zt, zt, ACT.Tanh).then_inc(s["tok_tanh"], 1)
                act.wait_ge(s["tok_sub"], p + 1)
                nc.scalar.activation(sc[:, :, :], sc[:, :, :], ACT.Exp).then_inc(s["tok_exp"], 1)
                act.wait_ge(s["tok_var"], p + 1)
                nc.scalar.activation(small[0:HT, 4, 0:4], small[0:HT, 3, 0:4], ACT.Sqrt).then_inc(s["tok_sqrt"], 1)

            def copy_sims(q):
                act.wait_ge(s["sims_ready"], q + 2)
                act.wait_ge(s["topk_done"], q + 1)
                nc.scalar.copy(sim[:, 0:512], b5[0:HT, :])
                nc.scalar.copy(sim[:, 512:1024], b6[0:HT, :]).then_inc(s["sims_read"], 1)

            def exp_kept(q):
                act.wait_ge(s["fin_sub"], q + 1)
                nc.scalar.activation(ff[:, :, :], ff[:, :, :], ACT.Exp).then_inc(s["fin_exp"], 1)

            def causal(c, k, slot):
                if slot >= 2 and (slot - 2) % 4 == 0 and slot < STEPS:
                    hp = (slot - 2) // 4
                    act.wait_ge(s["c_filled"], c * FILLS + 4 * hp + 1)
                    nc.scalar.activation(qk[:, :, :], b7[:, 0:2 * HT].rearrange("p (a n) -> p a n", a=2),
                                         ACT.Copy, scale=0.125).then_inc(s["c_read"], 1)
                if slot >= 3 and (slot - 3) % 4 == 0 and slot < STEPS:
                    hp = (slot - 3) // 4
                    act.wait_ge(s["c_neg"], 4 * c + hp + 1)
                    for a in range(2):
                        ins = nc.scalar.activation(sm[:, a, :], sm[:, a, :], ACT.Exp,
                                                   bias=small[0:HT, 10, a:a + 1], accum_out=small[0:HT, 11, a:a + 1])
                    ins.then_inc(s["c_exp"], 1)
                if slot >= 4 and slot % 4 == 0:
                    hp = slot // 4 - 1
                    act.wait_ge(s["c_filled"], c * FILLS + 4 * hp + 3)
                    nc.scalar.copy(pt[:, :, :], b7[0:HT, 0:4 * HT].rearrange("p (a n) -> p a n", a=4))\
                        .then_inc(s["c_read"], 1)
                if slot >= 5 and (slot - 5) % 4 == 0:
                    hp = (slot - 5) // 4
                    act.wait_ge(s["c_filled"], c * FILLS + 4 * hp + 4)
                    act.sem_inc(s["act_passed"], 1)
                    nc.scalar.activation(ott[:, 2 * hp:2 * hp + 2, :], b7[:, 0:2 * HT].rearrange("p (a n) -> p a n", a=2),
                                         ACT.Copy, scale=con[:, bass.ds(C_BATCH + k, 1)]).then_inc(s["c_read"], 1)

            def blk(p, k, now, keys, sums, back2):
                n, q, c = BLOCKS * p + k, 4 * (p - 1) + k + 1, 4 * (p - 2) + k
                for j in range(STEPS):
                    if now:
                        act.wait_ge(s["quad_free"], n * STEPS + j + 1)
                        for g in range(ACT_QUAD[j % 2]):
                            ins = nc.scalar.activation(d[:, j % RING, g, :], qp[:, :, :].rearrange("p h n -> p (h n)"),
                                                       ACT.Relu, bias=nx1t[:, bass.ds(k * BT + g * STEPS + j, 1)])
                        ins.then_inc(s["quad_act"], 1)
                    if keys and j == 0:
                        if now:
                            act.wait_ge(s["av_ready"], n + 1)
                        copy_sims(q)
                    if keys and j == KEYS_EXP:
                        exp_kept(q)
                    if back2:
                        causal(c, k, j)
                if back2:
                    causal(c, k, STEPS)
                if now:
                    act.wait_ge(s["s_ready"], n + 1)
                    act.wait_ge(s["v_done"], n + 1)
                    act.wait_ge(s["av_ready"], n + 1)
                    if keys:
                        act.wait_ge(s["topk_done"], q + 2)
                    for h in range(H):
                        ins = nc.scalar.activation(e[:, h, :], s_of(h), ACT.Exp, bias=bt[:, h:h + 1],
                                                   accum_out=z[:, 0, h:h + 1])
                    ins.then_inc(s["exps_done"], 1)
                if back2:
                    causal(c, k, STEPS + 1)
                if now:
                    for i in range(4):
                        act.wait_ge(s["at_filled"], 4 * n + i + 1)
                        src = (b5 if i % 2 == 0 else b6)[0:HT, :].rearrange("p (a r) -> p a r", a=4)
                        nc.scalar.copy(at[0:HT, 4 * i:4 * i + 4, :], src).then_inc(s["at_read"], 1)

            def iteration(p, now, back1, back2):
                if now:
                    tok(p)
                    act.wait_ge(s["vf_done"], p + 1)
                run_blocks(act, p, blk, now, back1, back2)
                if now:
                    act.wait_ge(s["ot_added"], BLOCKS * (p + 1) + 1)
                    nc.scalar.activation(th, ot[:, 0:NW], ACT.Tanh, scale=0.851).then_inc(s["o_tanh"], 1)
                    act.wait_ge(s["post_var"], p + 1)
                    nc.scalar.activation(small[0:HT, 9, 0:4], small[0:HT, 8, 0:4], ACT.Sqrt).then_inc(s["post_sqrt"], 1)
                    copy_sims(4 * p)
                    exp_kept(4 * p)
                if back1:
                    for i in range(4):
                        act.wait_ge(s["kt_filled"], 4 * (p - 1) + i + 1)
                        nc.scalar.copy(kt[:, 2 * i:2 * i + 2, :].rearrange("p h n -> p (h n)"), b7[:, 0:2 * NW])\
                            .then_inc(s["kt_read"], 1)

            run(act, iteration)

        @block.tensor
        def _(pe):
            mm, tr = nc.tensor.matmul, nc.tensor.transpose
            pe.wait_ge(s["w_loaded"], 16 * len(wd))
            for g in range(4):
                ins = mm(psum[:, g // 2, 256 * (g % 2):256 * (g % 2) + 256], wpk_sb[:, g, :],
                         pkb[:, g, :, :].rearrange("p h k -> p (h k)"), start=True, stop=True)
            ins.then_inc(s["setup_wc"], 1)
            pe.wait_ge(s["setup_done"], 1)
            pe.sem_inc(s["quad_free"], RING)

            def tok(p, back1):
                pe.wait_ge(s["x_loaded"], 80 * (p + 1))
                if back1:
                    pe.wait_ge(s["sims_read"], 4 * (p - 1) + 2)
                mm(b5[:, 0:NW], wqry2[:, :], xt[:, WIN // 2:WIN // 2 + NW], start=True, stop=True)
                mm(b6[:, 0:L], wkey2[:, :], xt[:, :], start=True, stop=True).then_inc(s["tok_proj"], 1)
                pe.wait_ge(s["tok_tanh"], p + 1)
                for half in range(2):
                    for w in range(WIN):
                        o = b5[0:HT, 0:4 * WIN].rearrange("p (a b s) -> p a b s", a=2, b=2)[:, half, :, w]
                        ins = mm(o, zt[:, w * NW + half * HT:w * NW + half * HT + HT], vblk[:, :], start=True, stop=True)
                ins.then_inc(s["tok_scores"], 1)

            def prep(p):
                pe.wait_ge(s["x1_done"], p + 1)
                for half in range(2):
                    ins = tr(b6[:, half * HT:half * HT + HT],
                             x1[:, 2 * half:2 * half + 2, :].rearrange("p b c -> p (b c)"), ident[0:HT, 0:HT])
                ins.then_inc(s["x1t_ready"], 1)
                pe.wait_ge(s["prep_done"], p + 1)
                pe.wait_ge(s["exps_done"], BLOCKS * p + 1)
                for h in range(H):
                    ins = mm(s_of(h), wqh[:, h, :], x1t[:, 0:NW], start=True, stop=True)
                ins.then_inc(s["q_ready"], 1)
                pe.wait_ge(s["q_read"], p + 1)
                for half in range(2):
                    for i in range(2):
                        ins = mm(psum[0:HT, 2 * half + i, :], x1t[:, half * HT:half * HT + HT],
                                 wvf[:, 4 * i:4 * i + 4, :, :].rearrange("p h b w -> p (h b w)"), start=True, stop=True)
                ins.then_inc(s["vf_ready"], 1)

            def sims(q):
                pe.wait_ge(s["xk_ready"], q + 1)
                mm(b5[0:HT, :], xk[:, :], wc[:, 0:512], start=True, stop=True)
                mm(b6[0:HT, :], xk[:, :], wc[:, 512:1024], start=True, stop=True).then_inc(s["sims_ready"], 1)

            def causal(p, c, k, j):
                hp, part_ = j // 4, j % 4
                pe.wait_ge(s["c_read"], c * FILLS + j + 1)
                if part_ == 0:
                    if j == 0:
                        pe.wait_ge(s["kt_read"], 4 * (p - 1) + 1)
                    for a in range(2):
                        ins = mm(b7[:, a * HT:a * HT + HT], wq2[:, 2 * hp + a, :],
                                 xmp[:, bass.ds(k, 1), :].rearrange("p a n -> p (a n)"), start=True, stop=True)
                elif part_ == 1:
                    for a in range(2):
                        ins = mm(b7[0:HT, a * NW:a * NW + NW], qk[:, a, :], kt[:, 2 * hp + a, :], start=True, stop=True)
                elif part_ == 2:
                    pe.wait_ge(s["c_norm"], 4 * c + hp + 1)
                    for a in range(2):
                        for jh in range(2):
                            c0 = (2 * a + jh) * HT
                            ins = tr(b7[0:HT, c0:c0 + HT], sm[:, a, jh * HT:jh * HT + HT], ident[0:HT, 0:HT])
                else:
                    for a in range(2):
                        for jh in range(2):
                            ins = mm(b7[:, a * HT:a * HT + HT], vv[:, jh, 2 * hp + a, :, :].rearrange("p b w -> p (b w)"),
                                     pt[:, 2 * a + jh, :], start=(jh == 0), stop=(jh == 1))
                ins.then_inc(s["c_filled"], 1)

            def blk(p, k, now, keys, sums, back2):
                n, q, c = BLOCKS * p + k, 4 * (p - 1) + k + 1, 4 * (p - 2) + k
                if keys:
                    if now:
                        pe.wait_ge(s["at_read"], 4 * n + 1)
                    pe.wait_ge(s["sims_read"], q + 1)
                    sims(q)
                if now:
                    pe.wait_ge(s["vf_done"], p + 1)
                    pe.wait_ge(s["exps_done"], n + 1)
                    for h in range(H):
                        for g in range(GR):
                            mm(s_of(h, slice(32 * g, 32 * g + 32)), acor[:, h, :, :].rearrange("p b j -> p (b j)"),
                               qp[:, h, :], start=(h % 2 == 0), stop=False, skip_group_check=True)
                for j in range(STEPS):
                    if now:
                        pe.wait_ge(s["quad_act"], n * STEPS + j + 1)
                        pe.wait_ge(s["quad_dve"], n * STEPS + j + 1)
                        for h in range(H):
                            for g in range(GR):
                                ins = mm(s_of(h, slice(32 * g, 32 * g + 32)), wpat[:, h, 15 - j:47 - j],
                                         d[:, j % RING, g, h * NW:h * NW + NW],
                                         start=False, stop=(j == STEPS - 1), skip_group_check=True)
                        ins.then_inc(s["quad_free"], 1)
                        if j == VB_FILL:
                            pe.wait_ge(s["x2k_ready"], n + 1)
                            if keys:
                                pe.wait_ge(s["sims_read"], q + 2)
                            else:
                                pe.wait_ge(s["at_read"], 4 * n + 1)
                            x2f = x2k[:, :, :, :].rearrange("p g b j -> p (g b j)")
                            mm(b6[:, :], x2f, wvb[:, :], start=True, stop=True)
                            mm(b5[:, 0:H], x2f, wk_s[:, 1, :], start=True, stop=True).then_inc(s["v_ready"], 1)
                        if j == STEPS - 1:
                            pe.wait_ge(s["quad_free"], n * STEPS + STEPS + RING)
                            pe.sem_inc(s["s_ready"], 1)
                    if back2:
                        causal(p, c, k, j)
                if back2:
                    pe.wait_ge(s["c_read"], c * FILLS + STEPS + 1)
                    for h in range(H):
                        ins = mm(b7[0:HT, 0:C], ott[:, h, :], wo2[:, h, :], start=(h == 0), stop=(h == H - 1))
                    ins.then_inc(s["c_filled"], 1)
                if not now:
                    return
                pe.wait_ge(s["attn_norm"], n + 1)
                for i in range(4):
                    bank = b5 if i % 2 == 0 else b6
                    if i >= 2:
                        pe.wait_ge(s["at_read"], 4 * n + i)
                    for a in range(4):
                        h, half = 2 * i + a // 2, a % 2
                        ins = tr(bank[0:HT, a * P:a * P + P], e[:, h, half * HT:half * HT + HT], ident)
                    ins.then_inc(s["at_filled"], 1)
                pe.wait_ge(s["ot_added"], n + 1)
                for h in range(H):
                    mm(b4[:, 0:NW], vbs[:, h, :, :].rearrange("p b w -> p (b w)"), e[:, h, :],
                       start=(h == 0), stop=(h == H - 1))
                pe.wait_ge(s["at_read"], 4 * n + 4 + 1)
                for h in range(H):
                    for half in range(2):
                        ins = mm(b4[:, 256:384], vf[:, half, h * P:h * P + P], at[0:HT, 2 * h + half, :],
                                 start=(h == 0 and half == 0), stop=(h == H - 1 and half == 1))
                ins.then_inc(s["av_ready"], 1)

            def iteration(p, now, back1, back2):
                if now:
                    tok(p, back1)
                    prep(p)
                run_blocks(pe, p, blk, now, back1, back2)
                if now:
                    pe.wait_ge(s["og_ready"], p + 1)
                    for half in range(2):
                        ins = mm(b5[0:HT, half * P:half * P + P], og[:, half * HT:half * HT + HT], fan2[:, :],
                                 start=True, stop=True)
                    ins.then_inc(s["y_ready"], 1)
                    pe.wait_ge(s["x2_done"], p + 1)
                    for half in range(2):
                        ins = tr(b6[:, half * HT:half * HT + HT],
                                 x2[:, 2 * half:2 * half + 2, :].rearrange("p b c -> p (b c)"), ident[0:HT, 0:HT])
                    ins.then_inc(s["x2t_ready"], 1)
                    sims(4 * p)
                if back1:
                    pe.wait_ge(s["kc_ready"], p)
                    if back2:
                        pe.wait_ge(s["c_read"], 4 * FILLS * (p - 1) + 1)
                    for i in range(4):
                        pe.wait_ge(s["kt_read"], 4 * (p - 1) + i + 1)
                        for a in range(2):
                            for half in range(2):
                                ins = tr(b7[:, a * NW + half * HT:a * NW + half * HT + HT],
                                         kc[:, half, 2 * i + a, :, :].rearrange("p b c -> p (b c)"), ident[0:HT, 0:HT])
                        ins.then_inc(s["kt_filled"], 1)

            run(pe, iteration)

        @block.vector
        def _(dve):
            V = nc.vector
            for tile in (wkey2[:, :], wqry2[:, :], vblk[:, :], wqh[:, :, :], wvf[:, :, :, :], fan2[:, :], wq2[:, :, :],
                         pkb):
                V.memset(tile, 0.0).then_inc(s["zeroed"], 1)
            ch = Chain(dve, s["setup_dve"], SETUP_LINKS)
            ch.begin(0)
            for tile in (wpat[:, :, :], acor[:, :, :, :], x1t[:, :], nx1t[:, :], x2k[:, :, :, :], vbs[:, :, :, :]):
                ch.link(V.memset(tile, 0.0))
            dve.wait_ge(s["w_loaded"], 16 * len(wd))
            ch.wait()
            ch.step(V.scalar_tensor_tensor(out=wk_s[:, 0, :], in0=wkt[:, :], scalar=-1.0, in1=wkt[:, :],
                                           op0=ALU.mult, op1=ALU.max))
            ch.step(V.tensor_scalar(wk_s[:, 0, :], wk_s[:, 0, :], TINY, None, ALU.max))
            ch.link(V.tensor_scalar(wk_s[:, 1, :], wk_s[:, 0, :], -0.125, None, ALU.mult))
            ch.link(V.tensor_scalar(wk_s[:, 2, :], wk_s[:, 0, :], 0.125, None, ALU.mult))
            ch.step(V.tensor_scalar(wk_s[:, 3, :], wkt[:, :], 0.0, 2.0, ALU.is_ge, ALU.mult))
            ch.step(V.tensor_scalar(wk_s[:, 3, :], wk_s[:, 3, :], -1.0, None, ALU.add))
            ch.step(V.tensor_tensor(wk_s[:, 3, :], wk_s[:, 3, :], wk_s[:, 0, :], ALU.mult))
            ch.step(V.reciprocal(wk_s[:, 4, :], wk_s[:, 3, :]))
            for b, r in enumerate(both):
                c0 = 15 + 16 * b
                ch.link(V.tensor_scalar(wpat[r, :, c0:c0 + 1], wk_s[r, 0, :].unsqueeze(2), -0.25, None, ALU.mult))
                ch.link(V.tensor_copy(acor[r, :, b, :], wk_s[r, 2, :].unsqueeze(2).to_broadcast([C, H, STEPS])))
            ch.step(V.tensor_scalar(fan2[:, :], fan2[:, :], 0.5, None, ALU.mult))
            ch.end()
            dve.wait_ge(s["wc_ready"], 1)
            for n in CREDITED:
                dve.sem_inc(s[n], 1)
            dve.sem_inc(s["slot_free"], SLOTS)
            dve.sem_inc(s["setup_done"], 1)

            def var_of(src, row, cn):
                a, b = small[0:HT, row, 0:4], small[0:HT, row + 1, 0:4]
                cn.step(V.tensor_reduce(a, src, AX.X, ALU.add))
                cn.step(V.tensor_scalar(a, a, 1.0 / C, None, ALU.mult))
                cn.step(V.tensor_tensor(cen[:, :, :], src, a.unsqueeze(2).to_broadcast([HT, 4, C]), ALU.subtract))
                cn.step(V.tensor_tensor(sq[:, :, :], cen[:, :, :], cen[:, :, :], ALU.mult))
                cn.step(V.tensor_reduce(b, sq[:, :, :], AX.X, ALU.add))

            sumc = Chain(dve, s["sum_dve"], SUM_LINKS)

            def weigh(p, u):
                at_u, slot = (u, u % SLOTS) if isinstance(u, int) else (u[0] + u[1], u[0] % SLOTS)
                cn = sumc
                cn.begin(p * UNITS + at_u)
                dve.wait_ge(loaded[slot], (p * UNITS + at_u - slot) * (16 * TOP // SLOTS) + 16 * TOP)
                g = g_rows[:, slot, :, :]
                w = wt[:, bass.ds(at_u * TOP, TOP)]
                cn.step(V.tensor_tensor(g, g, w.unsqueeze(2).to_broadcast([HT, TOP, 2 * C]), ALU.mult))
                V.tensor_reduce(kv[:, bass.ds(at_u * 2 * C, 2 * C)], g.rearrange("p m c -> p c m"), AX.X, ALU.add)\
                    .then_inc(s["slot_free"], 1)

            tokc = Chain(dve, s["tok_dve"], TOK_LINKS)

            def tok(p, back1):
                cn = tokc
                cn.begin(p)
                dve.wait_ge(s["tok_proj"], p + 1)
                cn.link(V.tensor_scalar(qry, b5[:, 0:NW], tokb[:, 0:1], None, ALU.add))
                cn.step(V.tensor_copy(key, b6[:, 0:L]))
                win = bass.AP(ring[:, :].tensor, key_at, [[RING * GR * H * NW, P], [1, WIN], [1, NW]])
                V.tensor_tensor(zt.rearrange("p (s w) -> p s w", s=WIN), win,
                                qry.unsqueeze(1).to_broadcast([P, WIN, NW]), ALU.add).then_inc(s["tok_z"], 1)
                if back1:
                    weigh(p - 1, 0)
                dve.wait_ge(s["tok_scores"], p + 1)
                scp = b5[0:HT, 0:4 * WIN].rearrange("p (a s) -> p a s", a=4)
                m = small[0:HT, 0, 0:4]
                cn.step(V.tensor_reduce(m, scp, AX.X, ALU.max))
                V.tensor_tensor(sc[:, :, :], scp, m.unsqueeze(2).to_broadcast([HT, 4, WIN]), ALU.subtract)\
                    .then_inc(s["tok_sub"], 1)
                dve.wait_ge(s["tok_exp"], p + 1)
                cn.step(V.tensor_reduce(small[0:HT, 1, 0:4], sc[:, :, :], AX.X, ALU.add))
                cn.step(V.reciprocal(small[0:HT, 1, 0:4], small[0:HT, 1, 0:4]))
                cn.step(V.tensor_tensor(sc[:, :, :], sc[:, :, :],
                                        small[0:HT, 1, 0:4].unsqueeze(2).to_broadcast([HT, 4, WIN]), ALU.mult))
                dve.wait_ge(s["x_loaded"], 80 * (p + 1))
                x3 = xw.rearrange("p (a c) -> p a c", c=C)
                cn.step(V.tensor_tensor(x3, x3, sc[:, :, :].rearrange("p a s -> p (a s)").unsqueeze(2)
                                        .to_broadcast([HT, 4 * WIN, C]), ALU.mult))
                V.tensor_reduce(h1, xw.rearrange("p (a s c) -> p a c s", a=4, s=WIN), AX.X, ALU.add)\
                    .then_inc(s["tok_done"], 1)
                dve.wait_ge(s["tok_done"], p + 2)
                var_of(h1, 2, cn)
                V.tensor_scalar(small[0:HT, 3, 0:4], small[0:HT, 3, 0:4], 1.0 / C, EPS, ALU.mult, ALU.add)\
                    .then_inc(s["tok_var"], 1)
                dve.wait_ge(s["tok_sqrt"], p + 1)
                r = small[0:HT, 5, 0:4]
                cn.step(V.reciprocal(r, small[0:HT, 4, 0:4]))
                V.tensor_tensor(x1, cen, r.unsqueeze(2).to_broadcast([HT, 4, C]), ALU.mult)\
                    .then_inc(s["x1_done"], 1)
                dve.wait_ge(s["x1_done"], p + 1)
                cn.step(V.tensor_tensor(hx[:, :, :], h1, x1, ALU.add))
                cn.step(V.tensor_tensor(hx[:, :, :], hx[:, :, :], fb[0:HT, :].unsqueeze(1).to_broadcast([HT, 4, C]),
                                        ALU.add))
                cn.end()

            prepc = Chain(dve, s["prep_dve"], PREP_LINKS)

            def prep(p, back1):
                cn = prepc
                cn.begin(p)
                dve.wait_ge(s["x1t_ready"], p + 1)
                cn.link(V.tensor_copy(x1t[:, 0:NW], b6[:, 0:NW]))
                cn.link(V.tensor_scalar(nx1t[:, 0:NW], b6[:, 0:NW], -1.0, None, ALU.mult))
                cn.wait()
                dve.sem_inc(s["prep_done"], 1)
                cn.link(V.memset(ot[:, :], 0.0))
                dve.wait_ge(s["q_ready"], p + 1)
                for h in range(H):
                    cn.link(V.tensor_scalar(qp[:, h, :], s_of(h), bq[:, h:h + 1], wk_s[:, 4, h:h + 1],
                                            ALU.add, ALU.mult))
                cn.wait()
                dve.sem_inc(s["q_read"], 1)
                if back1:
                    weigh(p - 1, 1)
                dve.wait_ge(s["vf_ready"], p + 1)
                for half in range(2):
                    for i in range(2):
                        hs = slice(4 * i * C, 4 * (i + 1) * C)
                        ins = V.tensor_tensor(
                            vf[:, half, i * 512:(i + 1) * 512].rearrange("p (h b w) -> p h b w", h=4, b=2),
                            psum[0:HT, 2 * half + i, :].rearrange("p (h b w) -> p h b w", h=4, b=2),
                            bvf[0:HT, hs].rearrange("p (h w) -> p h w", h=4).unsqueeze(2).to_broadcast([HT, 4, 2, C]),
                            ALU.add)
                        if half and i:
                            ins.then_inc(s["vf_done"], 1)
                        else:
                            cn.link(ins)
                cn.end()

            topc = Chain(dve, s["topk_dve"], TOPK_LINKS, s["dve_passed"])

            def take_tile(q, t):
                dve.wait_ge(s["sims_ready"], q + 1)
                V.tensor_copy(xk[:, :], xm[:, bass.ds(t, 1), :].rearrange("p a n -> p (a n)"))\
                    .then_inc(s["xk_ready"], 1)

            def topk(q, t):
                cn = topc
                cn.begin(q)
                dve.wait_ge(s["sims_read"], q + 2)
                dve.sem_inc(s["dve_passed"], 1)
                lists = [(sim[:, 64 * i:64 * i + 64], tv[:, i // H, i % H, :], ti[:, i // H, i % H, :])
                         for i in range(2 * H)]

                def top16(lists):
                    for lo in (0, 8):
                        for src, val, pos in lists:
                            cn.link(V.max(val[:, lo:lo + 8], src))
                        yield
                        cn.hold()
                        for src, val, pos in lists:
                            cn.link(V.max_index(pos[:, lo:lo + 8], val[:, lo:lo + 8], src))
                        yield
                        cn.hold()
                        if lo == 0:
                            for src, val, pos in lists:
                                cn.link(V.match_replace(src, val[:, 0:8], src, LOWEST))
                            yield
                            cn.hold()

                yield from top16(lists)
                cn.link(V.tensor_copy(code[:, 0, :, :], ti[:, 0, :, :]))
                hoff = con[0:HT, C_HOFF:C_END].rearrange("p (h m) -> p h m", h=H)
                cn.link(V.scalar_tensor_tensor(out=code[:, 1, :, :], in0=ti[:, 1, :, :], scalar=float(NK),
                                               in1=hoff, op0=ALU.mult, op1=ALU.add))

                def pairs_of(dst, src):
                    o = 0
                    for i0, ni, nj in TIES:
                        cn.link(V.tensor_tensor(
                            dst[:, :, o:o + ni * nj].rearrange("p h (i j) -> p h i j", i=ni),
                            src[:, 0, :, i0:i0 + ni].unsqueeze(3).to_broadcast([HT, H, ni, nj]),
                            src[:, 1, :, 0:nj].unsqueeze(2).to_broadcast([HT, H, ni, nj]), ALU.add))
                        o += ni * nj

                pairs_of(cs, tv)
                yield
                cn.wait()
                pairs_of(cc, code)
                yield
                cn.hold()
                yield from top16([(cs[:, h, :], fv[:, h, :], fi[:, h, :]) for h in range(H)])
                V.tensor_tensor(ff[:, :, :], fv[:, :, :], fv[:, :, 0:1].to_broadcast([HT, H, TOP]), ALU.subtract)\
                    .then_inc(s["fin_sub"], 1)
                cn.link(V.tensor_copy(keyf[:, :, :], fi[:, :, :]))
                iota = con[0:HT, C_IOTA:C_IOTA + CAND]
                eq3 = eq.rearrange("p (a c) -> p a c", c=CAND)
                eq4 = eq.rearrange("p (h m c) -> p h m c", h=2, c=CAND)
                for hg in range(H // 2):
                    yield
                    cn.wait()
                    kf = keyf[:, 2 * hg:2 * hg + 2, :].rearrange("p h m -> p (h m)")
                    cn.step(V.tensor_tensor(eq3, kf.unsqueeze(2).to_broadcast([HT, 2 * TOP, CAND]),
                                            iota.unsqueeze(1).to_broadcast([HT, 2 * TOP, CAND]), ALU.is_equal))
                    cn.step(V.tensor_tensor(eq4, eq4, cc[:, 2 * hg:2 * hg + 2, :].unsqueeze(2)
                                            .to_broadcast([HT, 2, TOP, CAND]), ALU.mult))
                    cn.link(V.tensor_reduce(kf, eq3, AX.X, ALU.add))
                yield
                cn.wait()
                V.tensor_copy(idx[:, bass.ds(t, 1), :].rearrange("p a m -> p (a m)"),
                              keyf[:, :, :].rearrange("p h m -> p (h m)")).then_inc(s["idx_ready"], 1)
                dve.wait_ge(s["fin_exp"], q + 1)
                zz = small[0:HT, 6, 0:H]
                cn.step(V.tensor_reduce(zz, ff[:, :, :], AX.X, ALU.add))
                cn.step(V.reciprocal(zz, zz))
                cn.step(V.tensor_tensor(wt[:, bass.ds(t * H * TOP, H * TOP)].rearrange("p (h m) -> p h m", h=H),
                                        ff[:, :, :], zz.unsqueeze(2).to_broadcast([HT, H, TOP]), ALU.mult))
                dve.sem_inc(s["topk_done"], 1)
                cn.end()

            cauc = Chain(dve, s["c_dve"], TILE_LINKS)

            def causal(c, k, slot):
                cn = cauc
                if slot == 0:
                    cn.begin(c)
                if slot >= 3 and (slot - 3) % 4 == 0 and slot < STEPS:
                    hp = (slot - 3) // 4
                    dve.wait_ge(s["c_filled"], c * FILLS + 4 * hp + 2)
                    mask = con[0:HT, bass.ds(C_MASK + k * NW, NW)]
                    cn.step(V.tensor_tensor(sm[:, :, :], b7[0:HT, 0:2 * NW].rearrange("p (a n) -> p a n", a=2),
                                            mask.unsqueeze(1).to_broadcast([HT, 2, NW]), ALU.add))
                    dve.sem_inc(s["c_read"], 1)
                    V.tensor_reduce(small[0:HT, 10, 0:2], sm[:, :, :], AX.X, ALU.max, negate=True).then_inc(s["c_neg"], 1)
                if slot >= 4 and slot % 4 == 0:
                    hp = slot // 4 - 1
                    dve.wait_ge(s["c_exp"], 4 * c + hp + 1)
                    cn.step(V.reciprocal(small[0:HT, 10, 2:4], small[0:HT, 11, 0:2]))
                    cn.link(V.tensor_scalar(sm[:, 0, :], sm[:, 0, :], small[0:HT, 10, 2:3], None, ALU.mult))
                    cn.step(V.tensor_scalar(sm[:, 1, :], sm[:, 1, :], small[0:HT, 10, 3:4], None, ALU.mult))
                    dve.sem_inc(s["c_norm"], 1)

            def causal_out(c, k):
                dve.wait_ge(s["c_filled"], (c + 1) * FILLS)
                V.tensor_tensor(outb[:, bass.ds(k, 1), :].rearrange("p a c -> p (a c)"), b7[0:HT, 0:C],
                                h2p[:, bass.ds(k, 1), :].rearrange("p a c -> p (a c)"), ALU.add)\
                    .then_inc(s["c_read"], 1)
                dve.wait_ge(s["c_read"], (c + 1) * FILLS + 1)
                dve.sem_inc(s["c_out"], 1)
                cauc.end()

            blkc = Chain(dve, s["blk_dve"], BLK_LINKS)

            def blk(p, k, now, keys, sums, back2):
                n, q, c = BLOCKS * p + k, 4 * (p - 1) + k + 1, 4 * (p - 2) + k
                cn = blkc
                unit = 0
                steps = iter(())
                if keys:
                    take_tile(q, k + 1)
                if now:
                    cn.begin(n)
                    dve.wait_ge(s["v_ready"], n + 1)
                    for b, r in enumerate(both):
                        ins = V.tensor_copy(x2k[r, :, b, :],
                                            x1t[r, bass.ds(k * BT, BT)].rearrange("p (g j) -> p g j", g=GR))
                        if b == 0:
                            cn.link(ins)
                    ins.then_inc(s["x2k_ready"], 1)
                for j in range(STEPS):
                    if now:
                        dve.wait_ge(s["quad_free"], n * STEPS + j + 1)
                        for g in range(ACT_QUAD[j % 2], GR):
                            ins = V.tensor_scalar(d[:, j % RING, g, :], qp[:, :, :].rearrange("p h n -> p (h n)"),
                                                  x1t[:, bass.ds(k * BT + g * STEPS + j, 1)], 0.0, ALU.subtract, ALU.max)
                        ins.then_inc(s["quad_dve"], 1)
                    if now and j == VB_FILL + 2:
                        dve.wait_ge(s["v_ready"], n + 2)
                        cn.link(V.tensor_copy(bt[:, :], b5[:, 0:H]))
                        cn.step(V.tensor_tensor(v1, b6[:, :].rearrange("p (h w) -> p h w", h=H),
                                                bvb[:, :].rearrange("p (h w) -> p h w", h=H), ALU.add))
                        for b in range(2):
                            ins = V.tensor_scalar(vbs[:, :, b, :], v1, con[:, bass.ds(C_ROWS + 2 * k + b, 1)],
                                                  None, ALU.mult)
                            if b == 0:
                                cn.link(ins)
                        ins.then_inc(s["v_done"], 1)
                        dve.wait_ge(s["v_done"], n + 1)
                    if back2:
                        causal(c, k, j)
                    if keys and j == 1:
                        steps = topk(q, k + 1)
                    if keys and j in KEYS_AT:
                        for _ in range(KEYS_AT[j]):
                            next(steps, None)
                    if sums and j in (UNIT_AT_LAST if isinstance(k, int) else UNIT_AT):
                        weigh(p - 1, (EARLY + unit, k * PER_BLOCK))
                        unit += 1
                if back2:
                    causal(c, k, STEPS)
                for _ in steps:
                    pass
                if now:
                    dve.wait_ge(s["exps_done"], n + 2)
                    cn.step(V.tensor_scalar(z[:, 1, :], z[:, 0, :], 1.0, None, ALU.add))
                    cn.step(V.reciprocal(z[:, 2, :], z[:, 1, :]))
                    for h in range(H):
                        ins = V.tensor_scalar(e[:, h, :], e[:, h, :], z[:, 2, h:h + 1], None, ALU.mult)
                        if h < H - 1:
                            cn.link(ins)
                    ins.then_inc(s["attn_norm"], 1)
                if back2:
                    causal_out(c, k)
                if now:
                    dve.wait_ge(s["av_ready"], n + 2)
                    cn.step(V.tensor_tensor(ot[:, 0:NW], ot[:, 0:NW], b4[:, 0:NW], ALU.add))
                    for b, r in enumerate(both):
                        o = ot[r, bass.ds(k * BT, BT)].rearrange("p (g j) -> p g j", g=GR)
                        ins = V.tensor_tensor(o, o, b4[r, 256:384].rearrange("p (g b j) -> p g b j", g=GR, b=2)[:, :, b, :],
                                              ALU.add)
                        if b == 0:
                            cn.step(ins)
                    ins.then_inc(s["ot_added"], 1)
                    cn.end()

            postc = Chain(dve, s["post_dve"], POST_LINKS)
            turnc = Chain(dve, s["turn_dve"], TURN_LINKS)

            def iteration(p, now, back1, back2):
                late = list(range(UNITS - LATE, UNITS)) if back1 else []
                if back2:
                    dve.wait_ge(s["stored"], 64 * (p - 2) + 1)
                if now:
                    tok(p, back1)
                    prep(p, back1)
                elif back1:
                    for u in range(EARLY):
                        weigh(p - 1, u)
                run_blocks(dve, p, blk, now, back1, back2)
                if back1:
                    cn = turnc
                    cn.begin(p - 1)
                    cn.link(V.tensor_copy(xmp[:, :, :], xm[:, :, :]))
                    cn.link(V.tensor_copy(h2p[:, :, :], h2[:, :, :]))
                    cn.wait()
                if now:
                    cn = postc
                    cn.begin(p)
                    dve.wait_ge(s["ot_added"], BLOCKS * (p + 1) + 1)
                    dve.wait_ge(s["o_tanh"], p + 1)
                    V.scalar_tensor_tensor(out=og, in0=th, scalar=1.0, in1=ot[:, 0:NW],
                                           op0=ALU.add, op1=ALU.mult).then_inc(s["og_ready"], 1)
                    if late:
                        weigh(p - 1, late.pop(0))
                    dve.wait_ge(s["y_ready"], p + 1)
                    cn.step(V.tensor_tensor(h2[:, :, :], b5[0:HT, 0:2 * P].rearrange("p (a c) -> p a c", a=4),
                                            hx[:, :, :], ALU.add))
                    var_of(h2[:, :, :], 7, cn)
                    V.tensor_scalar(small[0:HT, 8, 0:4], small[0:HT, 8, 0:4], 1.0 / C, EPS, ALU.mult, ALU.add)\
                        .then_inc(s["post_var"], 1)
                    dve.wait_ge(s["post_sqrt"], p + 1)
                    r = small[0:HT, 7, 0:4]
                    cn.step(V.reciprocal(r, small[0:HT, 9, 0:4]))
                    cn.step(V.tensor_tensor(x2, cen, r.unsqueeze(2).to_broadcast([HT, 4, C]), ALU.mult))
                    dve.sem_inc(s["x2_done"], 1)
                    dve.wait_ge(s["x2t_ready"], p + 1)
                    xm4 = xm[:, :, :].rearrange("p (f b) n -> p f b n", f=2)
                    for b in range(2):
                        cn.link(V.tensor_scalar(xm4[:, :, b, :], b6[:, 0:NW].rearrange("p (f n) -> p f n", f=2),
                                                con[:, C_BATCH + b:C_BATCH + b + 1], None, ALU.mult))
                    cn.wait()
                    cn.end()
                    take_tile(4 * p, 0)
                    for i, _ in enumerate(topk(4 * p, 0)):
                        if late and i % 5 == 4:
                            weigh(p - 1, late.pop(0))
                for u in late:
                    weigh(p - 1, u)
                if back1:
                    cn = turnc
                    dve.wait_ge(s["slot_free"], UNITS * p + SLOTS)
                    kv6 = kv[:, :].rearrange("p (f b h a c) -> p f b h a c", f=2, b=2, h=H, a=2)
                    for b in range(2):
                        cn.link(V.tensor_copy(kc[:, :, :, b, :], kv6[:, :, b, :, 0, :]))
                    cn.wait()
                    dve.sem_inc(s["kc_ready"], 1)
                    for b in range(2):
                        cn.link(V.tensor_copy(vv[:, :, :, b, :], kv6[:, :, b, :, 1, :]))
                    cn.wait()
                    cn.end()

            run(dve, iteration)


def kernel(x, L0_tok_W_qry, L0_tok_W_key, L0_tok_v, L0_tok_b, L0_attn_wqv_w, L0_attn_wqv_b, L0_attn_wk,
           L0_attn_fanin_w, L0_attn_fanin_b, L0_ffn_Wq_pk, L0_ffn_pk_keys, L0_ffn_Wq, L0_ffn_keys_table,
           L0_ffn_values_table, L0_ffn_Wo):
    import concourse.bacc as bacc
    from concourse.bass_utils import run_bass_kernel_spmd

    def a(t):
        return np.asarray(t)

    x = a(x)
    bias = a(L0_attn_wqv_b)
    arrays = {
        "x": x,
        "xT": x.transpose(0, 2, 1).reshape(PAIRS, 2 * C, L),
        "w_qry": a(L0_tok_W_qry), "w_key": a(L0_tok_W_key), "v_tok": a(L0_tok_v), "b_tok": a(L0_tok_b),
        "wqvT": a(L0_attn_wqv_w).T, "bqT": bias[:H * C].reshape(H, C).T, "b_qv": bias,
        "wkT": a(L0_attn_wk).T, "faninT": a(L0_attn_fanin_w).T, "b_fanin": a(L0_attn_fanin_b),
        "wpkT": a(L0_ffn_Wq_pk).T.reshape(4, P, C),
        "pkT": a(L0_ffn_pk_keys).transpose(0, 2, 3, 1).reshape(4, P, NK),
        "wq": a(L0_ffn_Wq),
        "tables": np.concatenate([a(L0_ffn_keys_table), a(L0_ffn_values_table)], axis=1),
        "wo": a(L0_ffn_Wo),
        "consts": constants(),
    }
    nc = bacc.Bacc("TRN2", target_bir_lowering=False, num_devices=1)
    ins, aps = {}, []
    for name, v in arrays.items():
        v = np.ascontiguousarray(v)
        ins[f"in_{name}"] = v
        aps.append(nc.dram_tensor(f"in_{name}", v.shape, mybir.dt.from_np(v.dtype), kind="ExternalInput").ap())
    out = nc.dram_tensor("out_h", (NB, NW, C), F32, kind="ExternalOutput").ap()
    build(nc, *aps, out)
    r = run_bass_kernel_spmd(nc, [ins], core_ids=[0])
    return r.results[0]["out_h"]
```

```python
from contextlib import ExitStack
from itertools import islice

import numpy as np

import concourse.bass as bass
from concourse import mybir

F32 = mybir.dt.float32
U32 = mybir.dt.uint32
ALU = mybir.AluOpType
ACT = mybir.ActivationFunctionType
AX = mybir.AxisListType

P = 128
NB, L, C = 16, 256, 64
WIN = 9
NW = L - WIN + 1
PAIRS = NB // 2
HT = NW // 2
H = 8
GR = 4
STEPS = 16
BT = GR * STEPS
BLOCKS = 4
RING = 2
NK = 64
TOP = 16
TIES = [(0, 1, 16), (1, 1, 8), (2, 3, 5), (5, 3, 2), (8, 8, 1)]
CAND = sum(n * m for _, n, m in TIES)
EPS = 1e-5
TINY = 1e-20
SLOTS = 2
UNITS = 4 * H
UNIT_AT = (1, 4, 7, 10, 13)
PER_BLOCK = len(UNIT_AT) + 2
REST_TOK = (BLOCKS - 1) * PER_BLOCK + 1
REST_BLOCK = REST_TOK + 3
ACT_QUAD = (2, 2) + (STEPS - 2) * (3,)
ACT_ALONE = STEPS * (2,)
QUERIES_AT = 5
SIMS_AT, VB_FILL = 0, 3
KEYS_AT = {2: 1, 3: 2, 4: 1, 5: 2, 6: 2, 7: 1, 8: 2, 9: 2, 11: 1, 12: 1, 14: 1, 15: 1}
KEYS_EXP = 12
KEYS_AT_FIRST = {2: 1, 3: 1, 4: 1, 5: 2, 6: 1, 7: 1, 8: 1, 9: 1, 11: 1, 12: 1, 14: 1}
KEYS_EXP_FIRST = 9
LOWEST = -3.0e38
MASKED = -1.0e30

C_ID = 0
C_MASK = P
C_ROWS = C_MASK + 4 * NW
C_BATCH = C_ROWS + 2 * BLOCKS
C_IOTA = C_BATCH + 4
C_HOFF = C_IOTA + CAND
C_END = C_HOFF + H * TOP


def constants():
    c = np.zeros((P, C_END), np.float32)
    c[:, C_ID:C_ID + P] = np.eye(P)
    i, j = np.arange(HT)[:, None], np.arange(HT)[None, :]
    for t in range(4):
        m = c[:HT, C_MASK + t * NW:C_MASK + (t + 1) * NW]
        m[:, t // 2 * HT:t // 2 * HT + HT] = np.where(j <= i, 0.0, MASKED)
        if t < 2:
            m[:, HT:] = MASKED
    r = np.arange(P)
    g, b, s = r // 32, r // 16 % 2, r % 16
    for k in range(BLOCKS):
        t = k * BT + g * STEPS + s
        for bb in range(2):
            c[:, C_ROWS + 2 * k + bb] = (b == bb) & (t < NW)
    for t in range(4):
        c[:, C_BATCH + t] = r // C == t % 2
    c[:, C_IOTA:C_IOTA + CAND] = np.arange(CAND)
    c[:, C_HOFF:C_END] = np.repeat(np.arange(H) * NK * NK, TOP)
    return c


class Chain:

    def __init__(self, eng, sem, per, passed=None):
        self.eng, self.sem, self.per, self.passed = eng, sem, per, passed

    def begin(self, instance):
        self.base, self.n = instance * self.per, 0

    def link(self, ins):
        self.n += 1
        ins.then_inc(self.sem, 1)

    def wait(self):
        self.eng.wait_ge(self.sem, self.base + self.n)

    def hold(self):
        self.wait()
        self.eng.sem_inc(self.passed, 1)

    def step(self, ins):
        self.link(ins)
        self.wait()

    def end(self):
        assert self.n == self.per, (self.sem, self.n)


TOK_LINKS, PREP_LINKS, BLK_LINKS, POST_LINKS, TOPK_LINKS, SUM_LINKS, TILE_LINKS, TURN_LINKS, SAVE_LINKS = 15, 14, 16, 10, 148, 1, 16, 4, 2
SETUP_LINKS = 19

CREDITED = ("tok_done", "exps_done", "av_ready", "topk_done", "sims_ready", "v_ready", "ot_added", "at_read",
            "sims_read", "c_masked", "c_turned", "ott_ready", "c_y", "y_read", "kt_read", "stored")


def build(nc, x, xT, w_qry, w_key, v_tok, b_tok, wqvT, bqT, b_qv, wkT, faninT, b_fanin,
          wpkT, pkT, wqT, tables, wo, consts, out):
    with ExitStack() as ctx:
        def sb(name, shape, dt=F32):
            return ctx.enter_context(nc.sbuf_tensor(name, shape, dt))

        def sem(name):
            return ctx.enter_context(nc.semaphore(name))

        psum = ctx.enter_context(nc.psum_tensor("psum", [P, 8, 512], F32))

        con = sb("con", [P, C_END])
        wkey2, wqry2 = sb("wkey2", [P, P]), sb("wqry2", [P, P])
        tokb = sb("tokb", [P, 1])
        vblk = sb("vblk", [P, 2])
        wqh = sb("wqh", [P, H, P])
        bq = sb("bq", [P, H])
        wkt = sb("wkt", [P, H])
        wk_s = sb("wk_s", [P, 5, H])
        wvf = sb("wvf", [P, H, 2, C])
        wvb = sb("wvb", [P, H * C])
        bvf, bvb = sb("bvf", [P, H * C]), sb("bvb", [P, H * C])
        fb = sb("fb", [P, C])
        fan2 = sb("fan2", [P, P])
        wq2 = sb("wq2", [P, H, P])
        wo2 = sb("wo2", [P, H, C])
        wc = sb("wc", [P, 2 * H * NK])
        wpat = sb("wpat", [P, H, 47])
        acor = sb("acor", [P, H, 2, STEPS])

        sc = sb("sc", [HT, 4, WIN])
        small = sb("small", [P, 12, 8])
        hx = sb("hx", [HT, 4, C])
        h2, h2p = sb("h2", [HT, 4, C]), sb("h2p", [HT, 4, C])
        xm, xmp = sb("xm", [P, 4, HT]), sb("xmp", [P, 4, HT])
        x1t, nx1t = sb("x1t", [P, BLOCKS * BT]), sb("nx1t", [P, BLOCKS * BT])
        qp = sb("qp", [P, H, NW])
        vf = sb("vf", [HT, 2, H * P])
        x2k = sb("x2k", [P, GR, 2, STEPS])
        bt = sb("bt", [P, H])
        vbs = sb("vbs", [P, H, 2, C])
        z = sb("z", [P, 3, H])
        ot = sb("ot", [P, BLOCKS * BT])
        xk = sb("xk", [P, HT])
        tv, ti = sb("tv", [HT, 2, H, TOP]), sb("ti", [HT, 2, H, TOP], U32)
        code = sb("code", [HT, 2, H, TOP])
        fv, fi = tv[:, 0, :, :], ti[:, 0, :, :]
        ff, keyf = code[:, 0, :, :], code[:, 1, :, :]
        idx = sb("idx", [HT, 4, H * TOP], U32)
        wt = sb("wt", [HT, 4 * H * TOP])
        g_rows = sb("g_rows", [HT, SLOTS, TOP, 2 * C])
        kv = sb("kv", [HT, 4 * H * 2 * C])
        vv = sb("vv", [HT, 2, H, 2, C])
        kt = sb("kt", [P, H, NW])
        xc = sb("xc", [P, HT])
        sm = sb("sm", [HT, 2, NW])
        pt = sb("pt", [HT, 4, HT])
        ott = sb("ott", [P, H, HT])
        outb = sb("outb", [HT, 4, C])
        e_keys = sb("e_keys", [P, H * NW])
        e = e_keys[:, :].rearrange("p (h n) -> p h n", h=H)
        sim = e_keys[0:HT, 0:2 * H * NK]
        cs = e_keys[0:HT, 1024:1024 + H * CAND].rearrange("p (h c) -> p h c", h=H)
        cc = e_keys[0:HT, 1024 + H * CAND:1024 + 2 * H * CAND].rearrange("p (h c) -> p h c", h=H)
        at_eq = sb("at_eq", [P, 2 * H * P])
        at = at_eq[:, :].rearrange("p (a n) -> p a n", n=P)
        v1 = at_eq[:, 0:H * C].rearrange("p (h w) -> p h w", w=C)
        eq = at_eq[0:HT, 0:2 * TOP * CAND]
        kc = at_eq[0:HT, :].rearrange("p (f h b c) -> p f h b c", f=2, h=H, b=2)
        kr = e

        ring = sb("ring", [P, RING * GR * H * NW])
        d = ring[:, :].rearrange("p (q g n) -> p q g n", q=RING, g=GR)
        at_ = [0]

        def part(n, rows=P):
            a = ring[0:rows, at_[0]:at_[0] + n]
            at_[0] += n
            return a
        xt = part(L)
        qry = part(NW)
        key_at = at_[0]
        key = part(L)
        zt = part(WIN * NW)
        xw = part(4 * WIN * C, HT)
        h1, x1, x2, cen, sq = (part(4 * C, HT).rearrange("p (a c) -> p a c", c=C) for _ in range(5))
        og, th = part(NW), part(NW)
        assert at_[0] <= RING * GR * H * NW
        wpk_sb = ring[:, 0:4 * P].rearrange("p (g c) -> p g c", g=4)
        pkb = ring[:, 4 * P:4 * P + 4 * 4 * NK].rearrange("p (g h k) -> p g h k", g=4, h=4)

        ident = con[:, C_ID:C_ID + P]
        S = psum[:, 0:4, 0:2 * NW].rearrange("p k (h n) -> p k h n", h=2)

        def s_of(h, rows=slice(0, P)):
            return S[rows, h // 2, h % 2, :]

        b4, b5, b6, b7 = (psum[:, k, :] for k in (4, 5, 6, 7))

        names = """zeroed w_loaded setup_dve setup_wc wc_ready setup_done
            x_loaded tok_proj tok_z tok_tanh tok_scores tok_sub tok_exp tok_var tok_sqrt tok_dve tok_done x1_done
            x1t_ready prep_done q_ready q_read vf_ready vf_done prep_dve
            x2k_ready v_ready v_done quad_act quad_dve quad_free s_ready exps_half exps_done norm_half attn_norm at_filled at_read
            av_ready ot_added blk_dve
            o_tanh og_ready y_ready post_var post_sqrt x2_done x2t_ready xm_ready post_dve
            xk_ready sims_ready sims_read topk_done fin_sub fin_exp idx_ready topk_dve
            dve_passed pool_passed sp_passed
            slot_free sum_dve
            h_saved save_dve kc_ready kt_filled kt_read turn_dve
            xc_ready c_scores c_masked c_neg c_exp c_norm c_turned pt_ready c_pv ott_ready c_y y_read c_out c_dve stored""".split()
        s = {n: sem(n) for n in names}
        loaded = [sem(f"slot{i}_loaded") for i in range(SLOTS)]

        ZEROS = 8
        both = [slice(0, C), slice(C, 2 * C)]
        wd = [(con[:, :], consts)]
        for b, r in enumerate(both):
            wd += [(wkey2[r, r], w_key), (wqry2[r, r], w_qry), (tokb[r, :], b_tok.unsqueeze(1)),
                   (vblk[r, b:b + 1], v_tok.unsqueeze(1)),
                   (wqh[r, :, r], wqvT[:, 0:512].rearrange("c (h w) -> c h w", h=H)),
                   (bq[r, :], bqT), (wkt[r, :], wkT),
                   (wvf[r, :, b, :], wqvT[:, 512:1024].rearrange("c (h w) -> c h w", h=H)),
                   (wvb[r, :], wqvT[:, 1024:1536]), (fan2[r, r], faninT),
                   (wq2[r, :, r], wqT.rearrange("(h w) c -> w h c", h=H)),
                   (wpk_sb[:, :, r], wpkT.rearrange("g p c -> p g c"))]
        wd += [(bvf[:, :], b_qv[512:1024].partition_broadcast(P)),
               (bvb[:, :], b_qv[1024:1536].partition_broadcast(P)),
               (fb[:, :], b_fanin.partition_broadcast(P))]
        wd += [(wo2[r, :, :], wo.rearrange("(h w) n -> w h n", h=H)) for r in both]
        wd += [(pkb[32 * a:32 * a + 32, :, a, :], pkT[:, 32 * a:32 * a + 32, :].rearrange("g p k -> p g k"))
               for a in range(4)]

        block = ctx.enter_context(nc.Block())

        def run(eng, iteration):
            iteration(0, now=True, keys=False, sums=False, rest=False, tiles=False, last=False)
            iteration(1, now=True, keys=True, sums=True, rest=False, tiles=False, last=False)
            iteration(2, now=True, keys=True, sums=True, rest=True, tiles=True, last=False)
            with eng.Fori(3, PAIRS) as p:
                iteration(p, now=True, keys=True, sums=True, rest=True, tiles=True, last=True)
            iteration(PAIRS, now=False, keys=True, sums=True, rest=True, tiles=True, last=True)
            iteration(PAIRS + 1, now=False, keys=False, sums=False, rest=True, tiles=True, last=True)
            iteration(PAIRS + 2, now=False, keys=False, sums=False, rest=False, tiles=False, last=True)

        @block.sync
        def _(sp):
            sp.wait_ge(s["zeroed"], ZEROS)
            for dst, src in wd:
                sp.dma_start(dst, src).then_inc(s["w_loaded"], 16)
            sp.wait_ge(s["setup_done"], 1)

            def iteration(p, now, keys, sums, rest, tiles, last):
                if now:
                    sp.wait_ge(s["tok_done"], p + 1)
                    sp.wait_ge(s["exps_done"], BLOCKS * p + 1)
                    sp.sem_inc(s["sp_passed"], 1)
                    sp.dma_start(xt, xT[bass.ds(p, 1), :, :].rearrange("a p l -> p (a l)"))\
                        .then_inc(s["x_loaded"], 16)
                    for hb in range(4):
                        half, b = hb // 2, hb % 2
                        src = bass.AP(x.tensor, p * (2 * L * C) + (b * L + half * HT) * C, [[C, HT], [1, WIN * C]])
                        sp.dma_start(xw[:, hb * WIN * C:(hb + 1) * WIN * C], src).then_inc(s["x_loaded"], 16)
                for k in range(BLOCKS):
                    if last if k == 0 else tiles:
                        t = (k - 1) % 4
                        sp.wait_ge(s["c_out"], 4 * (p - 2) + k)
                        sp.sem_inc(s["sp_passed"], 1)
                        half, b = t // 2, t % 2
                        pair = p - 3 if k == 0 else p - 2
                        sp.dma_start(out[bass.ds(2 * pair + b, 1), half * HT:(half + 1) * HT, :]
                                     .rearrange("a t c -> (a t) c"), outb[:, t, :]).then_inc(s["stored"], 16)

            run(sp, iteration)
            sp.wait_ge(s["stored"], 16 * 4 * PAIRS + 1)

        @block.gpsimd
        def _(pool):
            pool.wait_ge(s["setup_done"], 1)
            with pool.Fori(0, PAIRS) as p:
                for u in range(UNITS):
                    t, h = u // H, u % H
                    if h == 0:
                        pool.wait_ge(s["idx_ready"], 4 * p + t + 1)
                    pool.wait_ge(s["slot_free"], p * UNITS + u + 1)
                    pool.sem_inc(s["pool_passed"], 1)
                    for m in range(TOP):
                        nc.gpsimd.indirect_dma_start(
                            g_rows[:, u % SLOTS, m, :], None, tables,
                            bass.IndirectOffsetOnAxis(idx[:, t, h * TOP + m:h * TOP + m + 1], 0))\
                            .then_inc(loaded[u % SLOTS], 16)

        @block.scalar
        def _(act):
            act.wait_ge(s["setup_wc"], 1)
            nc.scalar.copy(wc[:, :].rearrange("p (a n) -> p a n", a=2), psum[:, 0:2, :]).then_inc(s["wc_ready"], 1)

            act.wait_ge(s["setup_done"], 1)

            def tok(p):
                act.wait_ge(s["tok_z"], p + 1)
                nc.scalar.activation(zt, zt, ACT.Tanh).then_inc(s["tok_tanh"], 1)
                act.wait_ge(s["tok_sub"], p + 1)
                nc.scalar.activation(sc[:, :, :], sc[:, :, :], ACT.Exp).then_inc(s["tok_exp"], 1)
                act.wait_ge(s["tok_var"], p + 1)
                nc.scalar.activation(small[0:HT, 4, 0:4], small[0:HT, 3, 0:4], ACT.Sqrt).then_inc(s["tok_sqrt"], 1)

            def copy_sims(q):
                act.wait_ge(s["sims_ready"], q + 2)
                act.wait_ge(s["topk_done"], q + 1)
                nc.scalar.copy(sim[:, 0:512], b5[0:HT, :])
                nc.scalar.copy(sim[:, 512:1024], b6[0:HT, :]).then_inc(s["sims_read"], 1)

            def exp_kept(q):
                act.wait_ge(s["fin_sub"], q + 1)
                nc.scalar.activation(ff[:, :, :], ff[:, :, :], ACT.Exp).then_inc(s["fin_exp"], 1)

            def causal_exp(c, hp):
                act.wait_ge(s["c_neg"], 4 * c + hp + 1)
                for a in range(2):
                    ins = nc.scalar.activation(sm[:, a, :], sm[:, a, :], ACT.Exp,
                                               bias=small[0:HT, 10, a:a + 1], accum_out=small[0:HT, 11, a:a + 1])
                ins.then_inc(s["c_exp"], 1)

            def causal_pt(c, hp):
                act.wait_ge(s["c_turned"], 4 * c + hp + 2)
                nc.scalar.copy(pt[:, :, :], b7[0:HT, 0:4 * HT].rearrange("p (a n) -> p a n", a=4))\
                    .then_inc(s["pt_ready"], 1)

            def causal_ott(c, t, hp):
                if hp == 0:
                    act.wait_ge(s["c_y"], c + 1)
                act.wait_ge(s["c_pv"], 4 * c + hp + 1)
                nc.scalar.activation(ott[:, 2 * hp:2 * hp + 2, :], b7[:, 0:2 * HT].rearrange("p (a n) -> p a n", a=2),
                                     ACT.Copy, scale=con[:, C_BATCH + t:C_BATCH + t + 1]).then_inc(s["ott_ready"], 1)

            def blk(p, k, now, keys, sums, causal, turn, last):
                n, q, c, t = BLOCKS * p + k, 4 * (p - 1) + k, 4 * (p - 2) + k - 1, (k - 1) % 4
                for j in range(STEPS):
                    if now:
                        act.wait_ge(s["quad_free"], n * STEPS + j + 1)
                        for g in range((ACT_QUAD if keys else ACT_ALONE)[j]):
                            ins = nc.scalar.activation(d[:, j % RING, g, :], qp[:, :, :].rearrange("p h n -> p (h n)"),
                                                       ACT.Relu, bias=nx1t[:, k * BT + g * STEPS + j:k * BT + g * STEPS + j + 1])
                        ins.then_inc(s["quad_act"], 1)
                    if j == 0 and now and (k > 1 and causal or k == 1 and last):
                        causal_ott(c - 1, t - 1 if k > 1 else 3, 3)
                    if turn and j == 0:
                        turn_keys(p - 2, keys and not now)
                    if keys and k and j == SIMS_AT + 1:
                        if now:
                            act.wait_ge(s["av_ready"], n + 1)
                        copy_sims(q)
                    if keys and j == (KEYS_EXP if k else KEYS_EXP_FIRST):
                        exp_kept(q)
                    if causal and j % 4 == 3:
                        causal_exp(c, j // 4)
                    if causal and j % 4 == 2 and j > 2:
                        causal_pt(c, j // 4 - 1)
                    if causal and j % 4 == 0 and j > 4:
                        causal_ott(c, t, j // 4 - 2)
                if causal:
                    causal_ott(c, t, 2)
                if now:
                    act.wait_ge(s["s_ready"], n + 1)
                    act.wait_ge(s["v_done"], n + 1)
                    act.wait_ge(s["av_ready"], n + 1)
                    if keys:
                        act.wait_ge(s["topk_done"], q + 2)
                    for h in range(H):
                        ins = nc.scalar.activation(e[:, h, :], s_of(h), ACT.Exp, bias=bt[:, h:h + 1],
                                                   accum_out=z[:, 0, h:h + 1])
                        if h == H // 2 - 1:
                            ins.then_inc(s["exps_half"], 1)
                    ins.then_inc(s["exps_done"], 1)
                if causal:
                    causal_pt(c, 3)
                if now:
                    for i in range(4):
                        act.wait_ge(s["at_filled"], 4 * n + i + 1)
                        src = (b5 if i % 2 == 0 else b6)[0:HT, :].rearrange("p (a r) -> p a r", a=4)
                        nc.scalar.copy(at[0:HT, 4 * i:4 * i + 4, :], src).then_inc(s["at_read"], 1)
                if causal and (k == BLOCKS - 1 or not now):
                    causal_ott(c, t, 3)

            def turn_keys(pair, alone):
                if alone:
                    act.wait_ge(s["topk_done"], 4 * pair + 4 + 2)
                for i in range(8):
                    act.wait_ge(s["kt_filled"], 8 * pair + i + 1)
                    dst = (kr if i < 4 else kt)[:, 2 * (i % 4):2 * (i % 4) + 2, :].rearrange("p h n -> p (h n)")
                    nc.scalar.activation(dst, (b7, b4)[i % 2][:, 0:2 * NW], ACT.Copy, scale=1.0 if i < 4 else 0.125)\
                        .then_inc(s["kt_read"], 1)

            def iteration(p, now, keys, sums, rest, tiles, last):
                if keys:
                    if now:
                        act.wait_ge(s["av_ready"], BLOCKS * p + 1)
                    copy_sims(4 * (p - 1))
                if now:
                    tok(p)
                    act.wait_ge(s["vf_done"], p + 1)
                for k in range(BLOCKS):
                    blk(p, k, now, keys, sums, tiles if k else last, tiles and k == 1, last)
                if now:
                    act.wait_ge(s["ot_added"], BLOCKS * (p + 1) + 1)
                    nc.scalar.activation(th, ot[:, 0:NW], ACT.Tanh, scale=0.851).then_inc(s["o_tanh"], 1)
                    act.wait_ge(s["post_var"], p + 1)
                    nc.scalar.activation(small[0:HT, 9, 0:4], small[0:HT, 8, 0:4], ACT.Sqrt).then_inc(s["post_sqrt"], 1)

            run(act, iteration)

        @block.tensor
        def _(pe):
            mm, tr = nc.tensor.matmul, nc.tensor.transpose
            pe.wait_ge(s["w_loaded"], 16 * len(wd))
            for g in range(4):
                ins = mm(psum[:, g // 2, 256 * (g % 2):256 * (g % 2) + 256], wpk_sb[:, g, :],
                         pkb[:, g, :, :].rearrange("p h k -> p (h k)"), start=True, stop=True)
            ins.then_inc(s["setup_wc"], 1)
            pe.wait_ge(s["setup_done"], 1)
            pe.sem_inc(s["quad_free"], RING)

            def tok(p, keys):
                pe.wait_ge(s["x_loaded"], 80 * (p + 1))
                if keys:
                    pe.wait_ge(s["sims_read"], 4 * (p - 1) + 2)
                mm(b5[:, 0:NW], wqry2[:, :], xt[:, WIN // 2:WIN // 2 + NW], start=True, stop=True)
                mm(b6[:, 0:L], wkey2[:, :], xt[:, :], start=True, stop=True).then_inc(s["tok_proj"], 1)
                pe.wait_ge(s["tok_tanh"], p + 1)
                for half in range(2):
                    for w in range(WIN):
                        o = b5[0:HT, 0:4 * WIN].rearrange("p (a b s) -> p a b s", a=2, b=2)[:, half, :, w]
                        ins = mm(o, zt[:, w * NW + half * HT:w * NW + half * HT + HT], vblk[:, :], start=True, stop=True)
                ins.then_inc(s["tok_scores"], 1)

            def prep(p):
                pe.wait_ge(s["x1_done"], p + 1)
                for half in range(2):
                    ins = tr(b6[:, half * HT:half * HT + HT],
                             x1[:, 2 * half:2 * half + 2, :].rearrange("p b c -> p (b c)"), ident[0:HT, 0:HT])
                ins.then_inc(s["x1t_ready"], 1)
                pe.wait_ge(s["prep_done"], p + 1)
                pe.wait_ge(s["exps_done"], BLOCKS * p + 1)
                for h in range(H):
                    ins = mm(s_of(h), wqh[:, h, :], x1t[:, 0:NW], start=True, stop=True)
                ins.then_inc(s["q_ready"], 1)
                pe.wait_ge(s["q_read"], p + 1)
                for half in range(2):
                    for i in range(2):
                        ins = mm(psum[0:HT, 2 * half + i, :], x1t[:, half * HT:half * HT + HT],
                                 wvf[:, 4 * i:4 * i + 4, :, :].rearrange("p h b w -> p (h b w)"), start=True, stop=True)
                ins.then_inc(s["vf_ready"], 1)

            def sims(q):
                pe.wait_ge(s["xk_ready"], q + 1)
                mm(b5[0:HT, :], xk[:, :], wc[:, 0:512], start=True, stop=True)
                mm(b6[0:HT, :], xk[:, :], wc[:, 512:1024], start=True, stop=True).then_inc(s["sims_ready"], 1)

            def causal_scores(n, c, hp, now):
                pe.wait_ge(s["c_masked"], 4 * c + hp + 1)
                if hp == 0:
                    if now:
                        pe.wait_ge(s["ot_added"], n + 1)
                    pe.wait_ge(s["xc_ready"], c + 1)
                for a in range(2):
                    ins = mm(b4[0:HT, a * NW:a * NW + NW], xc[:, :], kt[:, 2 * hp + a, :], start=True, stop=True)
                ins.then_inc(s["c_scores"], 1)

            def causal_turn(c, hp):
                pe.wait_ge(s["c_norm"], 4 * c + hp + 1)
                if hp == 0:
                    pe.wait_ge(s["y_read"], c + 1)
                pe.wait_ge(s["ott_ready"], 4 * c + hp + 1)
                for a in range(2):
                    for jh in range(2):
                        c0 = (2 * a + jh) * HT
                        ins = tr(b7[0:HT, c0:c0 + HT], sm[:, a, jh * HT:jh * HT + HT], ident[0:HT, 0:HT])
                ins.then_inc(s["c_turned"], 1)

            def causal_pv(c, hp):
                pe.wait_ge(s["pt_ready"], 4 * c + hp + 1)
                for a in range(2):
                    for jh in range(2):
                        ins = mm(b7[:, a * HT:a * HT + HT], vv[:, jh, 2 * hp + a, :, :].rearrange("p b w -> p (b w)"),
                                 pt[:, 2 * a + jh, :], start=(jh == 0), stop=(jh == 1))
                ins.then_inc(s["c_pv"], 1)

            def blk(p, k, now, keys, sums, causal, turn, last):
                n, q, c, t = BLOCKS * p + k, 4 * (p - 1) + k, 4 * (p - 2) + k - 1, (k - 1) % 4
                if now:
                    pe.wait_ge(s["vf_done"], p + 1)
                    pe.wait_ge(s["exps_done"], n + 1)
                for j in range(STEPS):
                    if now:
                        pe.wait_ge(s["quad_act"], n * STEPS + j + 1)
                        pe.wait_ge(s["quad_dve"], n * STEPS + j + 1)
                        for h in range(H):
                            for g in range(GR):
                                ins = mm(s_of(h, slice(32 * g, 32 * g + 32)), wpat[:, h, 15 - j:47 - j],
                                         d[:, j % RING, g, h * NW:h * NW + NW],
                                         start=(j == 0 and h % 2 == 0), stop=(j == STEPS - 1), skip_group_check=True)
                        ins.then_inc(s["quad_free"], 1)
                        if j == QUERIES_AT:
                            for h in range(H):
                                for g in range(GR):
                                    mm(s_of(h, slice(32 * g, 32 * g + 32)), acor[:, h, :, :].rearrange("p b j -> p (b j)"),
                                       qp[:, h, :], start=False, stop=False, skip_group_check=True)
                        if j == VB_FILL:
                            pe.wait_ge(s["x2k_ready"], n + 1)
                            if keys:
                                pe.wait_ge(s["sims_read"], q + 2)
                            if not (keys and k):
                                pe.wait_ge(s["at_read"], 4 * n + 1)
                            x2f = x2k[:, :, :, :].rearrange("p g b j -> p (g b j)")
                            mm(b6[:, :], x2f, wvb[:, :], start=True, stop=True)
                            mm(b5[:, 0:H], x2f, wk_s[:, 1, :], start=True, stop=True).then_inc(s["v_ready"], 1)
                        if j == STEPS - 1:
                            pe.wait_ge(s["quad_free"], n * STEPS + STEPS + RING)
                            pe.sem_inc(s["s_ready"], 1)
                    if turn and j == 0:
                        turn_keys(p - 2, n, now, last)
                    if keys and k and j == SIMS_AT:
                        if now:
                            pe.wait_ge(s["at_read"], 4 * n + 1)
                        pe.wait_ge(s["sims_read"], q + 1)
                        sims(q)
                    if causal and j % 4 == 0:
                        if j:
                            causal_turn(c, j // 4 - 1)
                        causal_scores(n, c, j // 4, now)
                    if causal and j % 4 == 2 and j > 2:
                        causal_pv(c, j // 4 - 1)
                if causal:
                    causal_turn(c, 3)
                if now:
                    attend(n)
                if causal:
                    causal_pv(c, 3)
                if now:
                    attend_back(n)
                if causal:
                    pe.wait_ge(s["ott_ready"], 4 * c + 4 + 1)
                    for h in range(H):
                        ins = mm(b7[0:HT, 0:C], ott[:, h, :], wo2[:, h, :], start=(h == 0), stop=(h == H - 1))
                    ins.then_inc(s["c_y"], 1)

            def attend(n):
                pe.wait_ge(s["norm_half"], n + 1)
                for i in range(4):
                    if i == 2:
                        pe.wait_ge(s["attn_norm"], n + 1)
                    bank = b5 if i % 2 == 0 else b6
                    if i >= 2:
                        pe.wait_ge(s["at_read"], 4 * n + i)
                    for a in range(4):
                        h, half = 2 * i + a // 2, a % 2
                        ins = tr(bank[0:HT, a * P:a * P + P], e[:, h, half * HT:half * HT + HT], ident)
                    ins.then_inc(s["at_filled"], 1)
                pe.wait_ge(s["ot_added"], n + 1)
                for h in range(H):
                    mm(b4[:, 0:NW], vbs[:, h, :, :].rearrange("p b w -> p (b w)"), e[:, h, :],
                       start=(h == 0), stop=(h == H - 1))

            def attend_back(n):
                pe.wait_ge(s["at_read"], 4 * n + 4 + 1)
                for h in range(H):
                    for half in range(2):
                        ins = mm(b4[:, 256:384], vf[:, half, h * P:h * P + P], at[0:HT, 2 * h + half, :],
                                 start=(h == 0 and half == 0), stop=(h == H - 1 and half == 1))
                ins.then_inc(s["av_ready"], 1)

            def turn_keys(pair, n, now, last):
                pe.wait_ge(s["kc_ready"], pair + 1)
                if last:
                    pe.wait_ge(s["y_read"], 4 * pair + 1)
                if now:
                    pe.wait_ge(s["ot_added"], n + 1)
                for i in range(8):
                    pe.wait_ge(s["kt_read"], 8 * pair + max(i, 1))
                    bank = (b7, b4)[i % 2]
                    for a in range(2):
                        h = 2 * (i % 4) + a
                        if i < 4:
                            for half in range(2):
                                ins = tr(bank[:, a * NW + half * HT:a * NW + half * HT + HT],
                                         kc[:, half, h, :, :].rearrange("p b c -> p (b c)"), ident[0:HT, 0:HT])
                        else:
                            ins = mm(bank[:, a * NW:a * NW + NW], wq2[:, h, :], kr[:, h, :], start=True, stop=True)
                    ins.then_inc(s["kt_filled"], 1)
                pe.wait_ge(s["kt_read"], 8 * pair + 8 + 1)

            def iteration(p, now, keys, sums, rest, tiles, last):
                if keys:
                    if now:
                        pe.wait_ge(s["xm_ready"], p)
                    pe.wait_ge(s["sims_read"], 4 * (p - 1) + 1)
                    sims(4 * (p - 1))
                if now:
                    tok(p, keys)
                    prep(p)
                for k in range(BLOCKS):
                    blk(p, k, now, keys, sums, tiles if k else last, tiles and k == 1, last)
                if now:
                    pe.wait_ge(s["og_ready"], p + 1)
                    for half in range(2):
                        ins = mm(b5[0:HT, half * P:half * P + P], og[:, half * HT:half * HT + HT], fan2[:, :],
                                 start=True, stop=True)
                    ins.then_inc(s["y_ready"], 1)
                    pe.wait_ge(s["x2_done"], p + 1)
                    for half in range(2):
                        ins = tr(b6[:, half * HT:half * HT + HT],
                                 x2[:, 2 * half:2 * half + 2, :].rearrange("p b c -> p (b c)"), ident[0:HT, 0:HT])
                    ins.then_inc(s["x2t_ready"], 1)

            run(pe, iteration)

        @block.vector
        def _(dve):
            V = nc.vector
            for tile in (wkey2[:, :], wqry2[:, :], vblk[:, :], wqh[:, :, :], wvf[:, :, :, :], fan2[:, :], wq2[:, :, :],
                         pkb):
                V.memset(tile, 0.0).then_inc(s["zeroed"], 1)
            ch = Chain(dve, s["setup_dve"], SETUP_LINKS)
            ch.begin(0)
            for tile in (wpat[:, :, :], acor[:, :, :, :], x1t[:, :], nx1t[:, :], x2k[:, :, :, :], vbs[:, :, :, :]):
                ch.link(V.memset(tile, 0.0))
            dve.wait_ge(s["w_loaded"], 16 * len(wd))
            ch.wait()
            ch.step(V.scalar_tensor_tensor(out=wk_s[:, 0, :], in0=wkt[:, :], scalar=-1.0, in1=wkt[:, :],
                                           op0=ALU.mult, op1=ALU.max))
            ch.step(V.tensor_scalar(wk_s[:, 0, :], wk_s[:, 0, :], TINY, None, ALU.max))
            ch.link(V.tensor_scalar(wk_s[:, 1, :], wk_s[:, 0, :], -0.125, None, ALU.mult))
            ch.link(V.tensor_scalar(wk_s[:, 2, :], wk_s[:, 0, :], 0.125, None, ALU.mult))
            ch.step(V.tensor_scalar(wk_s[:, 3, :], wkt[:, :], 0.0, 2.0, ALU.is_ge, ALU.mult))
            ch.step(V.tensor_scalar(wk_s[:, 3, :], wk_s[:, 3, :], -1.0, None, ALU.add))
            ch.step(V.tensor_tensor(wk_s[:, 3, :], wk_s[:, 3, :], wk_s[:, 0, :], ALU.mult))
            ch.step(V.reciprocal(wk_s[:, 4, :], wk_s[:, 3, :]))
            for b, r in enumerate(both):
                c0 = 15 + 16 * b
                ch.link(V.tensor_scalar(wpat[r, :, c0:c0 + 1], wk_s[r, 0, :].unsqueeze(2), -0.25, None, ALU.mult))
                ch.link(V.tensor_copy(acor[r, :, b, :], wk_s[r, 2, :].unsqueeze(2).to_broadcast([C, H, STEPS])))
            ch.step(V.tensor_scalar(fan2[:, :], fan2[:, :], 0.5, None, ALU.mult))
            ch.end()
            dve.wait_ge(s["wc_ready"], 1)
            for n in CREDITED:
                dve.sem_inc(s[n], 1)
            dve.sem_inc(s["slot_free"], SLOTS)
            dve.sem_inc(s["setup_done"], 1)

            def var_of(src, row, cn):
                a, b = small[0:HT, row, 0:4], small[0:HT, row + 1, 0:4]
                cn.step(V.tensor_reduce(a, src, AX.X, ALU.add))
                cn.step(V.tensor_scalar(a, a, 1.0 / C, None, ALU.mult))
                cn.step(V.tensor_tensor(cen[:, :, :], src, a.unsqueeze(2).to_broadcast([HT, 4, C]), ALU.subtract))
                cn.step(V.tensor_tensor(sq[:, :, :], cen[:, :, :], cen[:, :, :], ALU.mult))
                cn.step(V.tensor_reduce(b, sq[:, :, :], AX.X, ALU.add))

            sumc = Chain(dve, s["sum_dve"], SUM_LINKS)

            def weigh(p, u):
                cn = sumc
                cn.begin(p * UNITS + u)
                dve.wait_ge(loaded[u % SLOTS], (p * (UNITS // SLOTS) + u // SLOTS + 1) * 16 * TOP)
                g = g_rows[:, u % SLOTS, :, :]
                w = wt[:, u * TOP:(u + 1) * TOP]
                cn.step(V.tensor_tensor(g, g, w.unsqueeze(2).to_broadcast([HT, TOP, 2 * C]), ALU.mult))
                V.tensor_reduce(kv[:, u * 2 * C:(u + 1) * 2 * C], g.rearrange("p m c -> p c m"), AX.X, ALU.add)\
                    .then_inc(s["slot_free"], 1)

            tokc = Chain(dve, s["tok_dve"], TOK_LINKS)

            def tok(p, rest, steps):
                cn = tokc
                cn.begin(p)
                dve.wait_ge(s["tok_proj"], p + 1)
                cn.link(V.tensor_scalar(qry, b5[:, 0:NW], tokb[:, 0:1], None, ALU.add))
                cn.step(V.tensor_copy(key, b6[:, 0:L]))
                win = bass.AP(ring[:, :].tensor, key_at, [[RING * GR * H * NW, P], [1, WIN], [1, NW]])
                V.tensor_tensor(zt.rearrange("p (s w) -> p s w", s=WIN), win,
                                qry.unsqueeze(1).to_broadcast([P, WIN, NW]), ALU.add).then_inc(s["tok_z"], 1)
                if rest:
                    weigh(p - 2, REST_TOK)
                for _ in islice(steps, 2):
                    pass
                dve.wait_ge(s["tok_scores"], p + 1)
                scp = b5[0:HT, 0:4 * WIN].rearrange("p (a s) -> p a s", a=4)
                m = small[0:HT, 0, 0:4]
                cn.step(V.tensor_reduce(m, scp, AX.X, ALU.max))
                V.tensor_tensor(sc[:, :, :], scp, m.unsqueeze(2).to_broadcast([HT, 4, WIN]), ALU.subtract)\
                    .then_inc(s["tok_sub"], 1)
                dve.wait_ge(s["tok_exp"], p + 1)
                cn.step(V.tensor_reduce(small[0:HT, 1, 0:4], sc[:, :, :], AX.X, ALU.add))
                cn.step(V.reciprocal(small[0:HT, 1, 0:4], small[0:HT, 1, 0:4]))
                cn.step(V.tensor_tensor(sc[:, :, :], sc[:, :, :],
                                        small[0:HT, 1, 0:4].unsqueeze(2).to_broadcast([HT, 4, WIN]), ALU.mult))
                dve.wait_ge(s["x_loaded"], 80 * (p + 1))
                x3 = xw.rearrange("p (a c) -> p a c", c=C)
                cn.step(V.tensor_tensor(x3, x3, sc[:, :, :].rearrange("p a s -> p (a s)").unsqueeze(2)
                                        .to_broadcast([HT, 4 * WIN, C]), ALU.mult))
                V.tensor_reduce(h1, xw.rearrange("p (a s c) -> p a c s", a=4, s=WIN), AX.X, ALU.add)\
                    .then_inc(s["tok_done"], 1)
                dve.wait_ge(s["tok_done"], p + 2)
                var_of(h1, 2, cn)
                V.tensor_scalar(small[0:HT, 3, 0:4], small[0:HT, 3, 0:4], 1.0 / C, EPS, ALU.mult, ALU.add)\
                    .then_inc(s["tok_var"], 1)
                dve.wait_ge(s["tok_sqrt"], p + 1)
                r = small[0:HT, 5, 0:4]
                cn.step(V.reciprocal(r, small[0:HT, 4, 0:4]))
                V.tensor_tensor(x1, cen, r.unsqueeze(2).to_broadcast([HT, 4, C]), ALU.mult)\
                    .then_inc(s["x1_done"], 1)
                dve.wait_ge(s["x1_done"], p + 1)
                cn.step(V.tensor_tensor(hx[:, :, :], h1, x1, ALU.add))
                cn.step(V.tensor_tensor(hx[:, :, :], hx[:, :, :], fb[0:HT, :].unsqueeze(1).to_broadcast([HT, 4, C]),
                                        ALU.add))
                cn.end()

            prepc = Chain(dve, s["prep_dve"], PREP_LINKS)

            def prep(p, rest, steps):
                cn = prepc
                cn.begin(p)
                dve.wait_ge(s["x1t_ready"], p + 1)
                cn.link(V.tensor_copy(x1t[:, 0:NW], b6[:, 0:NW]))
                cn.link(V.tensor_scalar(nx1t[:, 0:NW], b6[:, 0:NW], -1.0, None, ALU.mult))
                cn.wait()
                dve.sem_inc(s["prep_done"], 1)
                cn.link(V.memset(ot[:, :], 0.0))
                if rest:
                    weigh(p - 2, REST_TOK + 1)
                for _ in islice(steps, 2):
                    pass
                dve.wait_ge(s["q_ready"], p + 1)
                for h in range(H):
                    cn.link(V.tensor_scalar(qp[:, h, :], s_of(h), bq[:, h:h + 1], wk_s[:, 4, h:h + 1],
                                            ALU.add, ALU.mult))
                cn.wait()
                dve.sem_inc(s["q_read"], 1)
                if rest:
                    weigh(p - 2, REST_TOK + 2)
                for _ in islice(steps, 2):
                    pass
                dve.wait_ge(s["vf_ready"], p + 1)
                for half in range(2):
                    for i in range(2):
                        hs = slice(4 * i * C, 4 * (i + 1) * C)
                        ins = V.tensor_tensor(
                            vf[:, half, i * 512:(i + 1) * 512].rearrange("p (h b w) -> p h b w", h=4, b=2),
                            psum[0:HT, 2 * half + i, :].rearrange("p (h b w) -> p h b w", h=4, b=2),
                            bvf[0:HT, hs].rearrange("p (h w) -> p h w", h=4).unsqueeze(2).to_broadcast([HT, 4, 2, C]),
                            ALU.add)
                        if half and i:
                            ins.then_inc(s["vf_done"], 1)
                        else:
                            cn.link(ins)
                cn.end()

            topc = Chain(dve, s["topk_dve"], TOPK_LINKS, s["dve_passed"])

            def take_tile(q, t):
                dve.wait_ge(s["sims_ready"], q + 1)
                V.tensor_copy(xk[:, :], xm[:, t, :])\
                    .then_inc(s["xk_ready"], 1)

            def topk(q, t):
                cn = topc
                cn.begin(q)
                dve.wait_ge(s["sims_read"], q + 2)
                dve.sem_inc(s["dve_passed"], 1)
                lists = [(sim[:, 64 * i:64 * i + 64], tv[:, i // H, i % H, :], ti[:, i // H, i % H, :])
                         for i in range(2 * H)]

                def top16(lists):
                    for lo in (0, 8):
                        for src, val, pos in lists:
                            cn.link(V.max(val[:, lo:lo + 8], src))
                        yield
                        cn.hold()
                        for src, val, pos in lists:
                            cn.link(V.max_index(pos[:, lo:lo + 8], val[:, lo:lo + 8], src))
                        yield
                        cn.hold()
                        if lo == 0:
                            for src, val, pos in lists:
                                cn.link(V.match_replace(src, val[:, 0:8], src, LOWEST))
                            yield
                            cn.hold()

                yield from top16(lists)
                cn.link(V.tensor_copy(code[:, 0, :, :], ti[:, 0, :, :]))
                hoff = con[0:HT, C_HOFF:C_END].rearrange("p (h m) -> p h m", h=H)
                cn.link(V.scalar_tensor_tensor(out=code[:, 1, :, :], in0=ti[:, 1, :, :], scalar=float(NK),
                                               in1=hoff, op0=ALU.mult, op1=ALU.add))

                def pairs_of(dst, src):
                    o = 0
                    for i0, ni, nj in TIES:
                        cn.link(V.tensor_tensor(
                            dst[:, :, o:o + ni * nj].rearrange("p h (i j) -> p h i j", i=ni),
                            src[:, 0, :, i0:i0 + ni].unsqueeze(3).to_broadcast([HT, H, ni, nj]),
                            src[:, 1, :, 0:nj].unsqueeze(2).to_broadcast([HT, H, ni, nj]), ALU.add))
                        o += ni * nj

                pairs_of(cs, tv)
                yield
                cn.wait()
                pairs_of(cc, code)
                yield
                cn.hold()
                yield from top16([(cs[:, h, :], fv[:, h, :], fi[:, h, :]) for h in range(H)])
                V.tensor_tensor(ff[:, :, :], fv[:, :, :], fv[:, :, 0:1].to_broadcast([HT, H, TOP]), ALU.subtract)\
                    .then_inc(s["fin_sub"], 1)
                cn.link(V.tensor_copy(keyf[:, :, :], fi[:, :, :]))
                iota = con[0:HT, C_IOTA:C_IOTA + CAND]
                eq3 = eq.rearrange("p (a c) -> p a c", c=CAND)
                eq4 = eq.rearrange("p (h m c) -> p h m c", h=2, c=CAND)
                for hg in range(H // 2):
                    yield
                    cn.wait()
                    kf = keyf[:, 2 * hg:2 * hg + 2, :].rearrange("p h m -> p (h m)")
                    cn.step(V.tensor_tensor(eq3, kf.unsqueeze(2).to_broadcast([HT, 2 * TOP, CAND]),
                                            iota.unsqueeze(1).to_broadcast([HT, 2 * TOP, CAND]), ALU.is_equal))
                    cn.step(V.tensor_tensor(eq4, eq4, cc[:, 2 * hg:2 * hg + 2, :].unsqueeze(2)
                                            .to_broadcast([HT, 2, TOP, CAND]), ALU.mult))
                    cn.link(V.tensor_reduce(kf, eq3, AX.X, ALU.add))
                yield
                cn.wait()
                V.tensor_copy(idx[:, t, :],
                              keyf[:, :, :].rearrange("p h m -> p (h m)")).then_inc(s["idx_ready"], 1)
                dve.wait_ge(s["fin_exp"], q + 1)
                zz = small[0:HT, 6, 0:H]
                cn.step(V.tensor_reduce(zz, ff[:, :, :], AX.X, ALU.add))
                cn.step(V.reciprocal(zz, zz))
                cn.step(V.tensor_tensor(wt[:, t * H * TOP:(t + 1) * H * TOP].rearrange("p (h m) -> p h m", h=H),
                                        ff[:, :, :], zz.unsqueeze(2).to_broadcast([HT, H, TOP]), ALU.mult))
                dve.sem_inc(s["topk_done"], 1)
                cn.end()

            cauc = Chain(dve, s["c_dve"], TILE_LINKS)

            def causal_mask(c, t, hp):
                cn = cauc
                dve.wait_ge(s["c_scores"], 4 * c + hp + 1)
                dve.wait_ge(s["c_turned"], 4 * c + hp + 1)
                mask = con[0:HT, C_MASK + t * NW:C_MASK + (t + 1) * NW]
                cn.step(V.tensor_tensor(sm[:, :, :], b4[0:HT, 0:2 * NW].rearrange("p (a n) -> p a n", a=2),
                                        mask.unsqueeze(1).to_broadcast([HT, 2, NW]), ALU.add))
                dve.sem_inc(s["c_masked"], 1)
                V.tensor_reduce(small[0:HT, 10, 0:2], sm[:, :, :], AX.X, ALU.max, negate=True).then_inc(s["c_neg"], 1)

            def causal_norm(c, hp):
                cn = cauc
                dve.wait_ge(s["c_exp"], 4 * c + hp + 1)
                cn.step(V.reciprocal(small[0:HT, 10, 2:4], small[0:HT, 11, 0:2]))
                cn.link(V.tensor_scalar(sm[:, 0, :], sm[:, 0, :], small[0:HT, 10, 2:3], None, ALU.mult))
                cn.step(V.tensor_scalar(sm[:, 1, :], sm[:, 1, :], small[0:HT, 10, 3:4], None, ALU.mult))
                dve.sem_inc(s["c_norm"], 1)

            def causal_out(c, t):
                dve.wait_ge(s["stored"], 16 * c + 1)
                dve.wait_ge(s["c_y"], c + 2)
                V.tensor_tensor(outb[:, t, :], b7[0:HT, 0:C], outb[:, t, :] if t == 3 else h2p[:, t, :], ALU.add)\
                    .then_inc(s["y_read"], 1)
                dve.wait_ge(s["y_read"], c + 2)
                dve.sem_inc(s["c_out"], 1)
                cauc.end()

            turnc = Chain(dve, s["turn_dve"], TURN_LINKS)

            def turn_keys(pair):
                cn = turnc
                cn.begin(pair)
                dve.wait_ge(s["slot_free"], UNITS * (pair + 1) + SLOTS)
                kv6 = kv[:, :].rearrange("p (f b h a c) -> p f b h a c", f=2, b=2, h=H, a=2)
                for b in range(2):
                    cn.link(V.tensor_copy(kc[:, :, :, b, :], kv6[:, :, b, :, 0, :]))
                cn.wait()
                dve.sem_inc(s["kc_ready"], 1)
                for b in range(2):
                    cn.link(V.tensor_copy(vv[:, :, :, b, :], kv6[:, :, b, :, 1, :]))
                cn.wait()
                cn.end()

            blkc = Chain(dve, s["blk_dve"], BLK_LINKS)

            def rectify(n, at, j, keys):
                dve.wait_ge(s["quad_free"], n * STEPS + j + 1)
                for g in range((ACT_QUAD if keys else ACT_ALONE)[j], GR):
                    ins = V.tensor_scalar(d[:, j % RING, g, :], qp[:, :, :].rearrange("p h n -> p (h n)"),
                                          x1t[:, at + g * STEPS + j:at + g * STEPS + j + 1], 0.0, ALU.subtract, ALU.max)
                ins.then_inc(s["quad_dve"], 1)

            def blk(p, k, now, keys, steps, sums, causal, turn):
                n, q, c, t = BLOCKS * p + k, 4 * (p - 1) + k, 4 * (p - 2) + k - 1, (k - 1) % 4
                cn = blkc
                sums = iter(sums)
                if turn:
                    turn_keys(p - 2)
                if keys and k:
                    take_tile(q, k)
                if causal:
                    cauc.begin(c)
                    if k:
                        V.tensor_copy(xc[:, :], xmp[:, t, :]).then_inc(s["xc_ready"], 1)
                if now:
                    cn.begin(n)
                    dve.wait_ge(s["v_ready"], n + 1)
                    for b, r in enumerate(both):
                        ins = V.tensor_copy(x2k[r, :, b, :],
                                            x1t[r, k * BT:(k + 1) * BT].rearrange("p (g j) -> p g j", g=GR))
                        if b == 0:
                            cn.link(ins)
                    ins.then_inc(s["x2k_ready"], 1)
                for j in range(STEPS):
                    if now and j >= RING:
                        rectify(n, k * BT, j, keys)
                    if now and j == VB_FILL + 2:
                        dve.wait_ge(s["v_ready"], n + 2)
                        cn.link(V.tensor_copy(bt[:, :], b5[:, 0:H]))
                        cn.step(V.tensor_tensor(v1, b6[:, :].rearrange("p (h w) -> p h w", h=H),
                                                bvb[:, :].rearrange("p (h w) -> p h w", h=H), ALU.add))
                        for b in range(2):
                            ins = V.tensor_scalar(vbs[:, :, b, :], v1, con[:, C_ROWS + 2 * k + b:C_ROWS + 2 * k + b + 1],
                                                  None, ALU.mult)
                            if b == 0:
                                cn.link(ins)
                        ins.then_inc(s["v_done"], 1)
                        dve.wait_ge(s["v_done"], n + 1)
                    if causal and j % 4 == 0 and j:
                        causal_norm(c, j // 4 - 1)
                    if keys and j == min(KEYS_AT) and k:
                        steps = topk(q, k)
                    for _ in islice(steps, (KEYS_AT if k else KEYS_AT_FIRST).get(j, 0)):
                        pass
                    if causal and j % 4 == 2:
                        causal_mask(c, t, j // 4)
                    if j in UNIT_AT:
                        for pair, u in islice(sums, 1):
                            weigh(pair, u)
                if causal:
                    causal_norm(c, 3)
                for _ in steps:
                    pass
                for pair, u in islice(sums, 1):
                    weigh(pair, u)
                if now:
                    for hs, done in ((slice(0, H // 2), "exps_half"), (slice(H // 2, H), "exps_done")):
                        dve.wait_ge(s[done], n + (2 if done in CREDITED else 1))
                        cn.step(V.tensor_scalar(z[:, 1, hs], z[:, 0, hs], 1.0, None, ALU.add))
                        cn.step(V.reciprocal(z[:, 2, hs], z[:, 1, hs]))
                        for h in range(hs.start, hs.stop):
                            ins = V.tensor_scalar(e[:, h, :], e[:, h, :], z[:, 2, h:h + 1], None, ALU.mult)
                            if h == H // 2 - 1:
                                ins.then_inc(s["norm_half"], 1)
                            elif h < H - 1:
                                cn.link(ins)
                    ins.then_inc(s["attn_norm"], 1)
                    if k < BLOCKS - 1:
                        for j in range(RING):
                            rectify(n + 1, k * BT + BT, j, keys)
                for pair, u in sums:
                    weigh(pair, u)
                if now:
                    dve.wait_ge(s["av_ready"], n + 2)
                    cn.step(V.tensor_tensor(ot[:, 0:NW], ot[:, 0:NW], b4[:, 0:NW], ALU.add))
                    for b, r in enumerate(both):
                        o = ot[r, k * BT:(k + 1) * BT].rearrange("p (g j) -> p g j", g=GR)
                        ins = V.tensor_tensor(o, o, b4[r, 256:384].rearrange("p (g b j) -> p g b j", g=GR, b=2)[:, :, b, :],
                                              ALU.add)
                        if b == 0:
                            cn.step(ins)
                    ins.then_inc(s["ot_added"], 1)
                    cn.end()
                if causal:
                    causal_out(c, t)

            postc = Chain(dve, s["post_dve"], POST_LINKS)

            savec = Chain(dve, s["save_dve"], SAVE_LINKS)

            def iteration(p, now, keys, sums, rest, tiles, last):
                steps = iter(())
                if keys:
                    take_tile(4 * (p - 1), 0)
                    steps = topk(4 * (p - 1), 0)
                if now:
                    tok(p, rest, steps)
                    prep(p, rest, steps)
                    for j in range(RING):
                        rectify(BLOCKS * p, 0, j, keys)
                elif rest:
                    for u in range(REST_TOK, REST_BLOCK):
                        weigh(p - 2, u)
                        for _ in islice(steps, 2):
                            pass
                for k in range(BLOCKS):
                    if k:
                        units = [(p - 1, (k - 1) * PER_BLOCK + i) for i in range(PER_BLOCK)] if sums else []
                    else:
                        units = [(p - 2, u) for u in range(REST_BLOCK, UNITS)] if rest else []
                    blk(p, k, now, keys, iter(()) if k else steps, units, tiles if k else last, tiles and k == 1)
                if tiles:
                    V.tensor_copy(xc[:, :], xmp[:, 3, :]).then_inc(s["xc_ready"], 1)
                    V.tensor_copy(outb[:, 3, :], h2p[:, 3, :]).then_inc(s["h_saved"], 1)
                    dve.wait_ge(s["h_saved"], p - 1)
                if keys:
                    cn = savec
                    cn.begin(p - 1)
                    cn.link(V.tensor_copy(xmp[:, :, :], xm[:, :, :]))
                    cn.link(V.tensor_copy(h2p[:, :, :], h2[:, :, :]))
                    cn.wait()
                    cn.end()
                if now:
                    cn = postc
                    cn.begin(p)
                    dve.wait_ge(s["ot_added"], BLOCKS * (p + 1) + 1)
                    dve.wait_ge(s["o_tanh"], p + 1)
                    V.scalar_tensor_tensor(out=og, in0=th, scalar=1.0, in1=ot[:, 0:NW],
                                           op0=ALU.add, op1=ALU.mult).then_inc(s["og_ready"], 1)
                    if sums:
                        weigh(p - 1, REST_TOK - 1)
                    dve.wait_ge(s["y_ready"], p + 1)
                    cn.step(V.tensor_tensor(h2[:, :, :], b5[0:HT, 0:2 * P].rearrange("p (a c) -> p a c", a=4),
                                            hx[:, :, :], ALU.add))
                    var_of(h2[:, :, :], 7, cn)
                    V.tensor_scalar(small[0:HT, 8, 0:4], small[0:HT, 8, 0:4], 1.0 / C, EPS, ALU.mult, ALU.add)\
                        .then_inc(s["post_var"], 1)
                    dve.wait_ge(s["post_sqrt"], p + 1)
                    r = small[0:HT, 7, 0:4]
                    cn.step(V.reciprocal(r, small[0:HT, 9, 0:4]))
                    cn.step(V.tensor_tensor(x2, cen, r.unsqueeze(2).to_broadcast([HT, 4, C]), ALU.mult))
                    dve.sem_inc(s["x2_done"], 1)
                    dve.wait_ge(s["x2t_ready"], p + 1)
                    xm4 = xm[:, :, :].rearrange("p (f b) n -> p f b n", f=2)
                    for b in range(2):
                        cn.link(V.tensor_scalar(xm4[:, :, b, :], b6[:, 0:NW].rearrange("p (f n) -> p f n", f=2),
                                                con[:, C_BATCH + b:C_BATCH + b + 1], None, ALU.mult))
                    cn.wait()
                    cn.end()
                    dve.sem_inc(s["xm_ready"], 1)
                elif sums:
                    weigh(p - 1, REST_TOK - 1)

            run(dve, iteration)


def kernel(x, L0_tok_W_qry, L0_tok_W_key, L0_tok_v, L0_tok_b, L0_attn_wqv_w, L0_attn_wqv_b, L0_attn_wk,
           L0_attn_fanin_w, L0_attn_fanin_b, L0_ffn_Wq_pk, L0_ffn_pk_keys, L0_ffn_Wq, L0_ffn_keys_table,
           L0_ffn_values_table, L0_ffn_Wo):
    import concourse.bacc as bacc
    from concourse.bass_utils import run_bass_kernel_spmd

    def a(t):
        return np.asarray(t)

    x = a(x)
    bias = a(L0_attn_wqv_b)
    arrays = {
        "x": x,
        "xT": x.transpose(0, 2, 1).reshape(PAIRS, 2 * C, L),
        "w_qry": a(L0_tok_W_qry), "w_key": a(L0_tok_W_key), "v_tok": a(L0_tok_v), "b_tok": a(L0_tok_b),
        "wqvT": a(L0_attn_wqv_w).T, "bqT": bias[:H * C].reshape(H, C).T, "b_qv": bias,
        "wkT": a(L0_attn_wk).T, "faninT": a(L0_attn_fanin_w).T, "b_fanin": a(L0_attn_fanin_b),
        "wpkT": a(L0_ffn_Wq_pk).T.reshape(4, P, C),
        "pkT": a(L0_ffn_pk_keys).transpose(0, 2, 3, 1).reshape(4, P, NK),
        "wqT": a(L0_ffn_Wq).T,
        "tables": np.concatenate([a(L0_ffn_keys_table), a(L0_ffn_values_table)], axis=1),
        "wo": a(L0_ffn_Wo),
        "consts": constants(),
    }
    nc = bacc.Bacc("TRN2", target_bir_lowering=False, num_devices=1)
    ins, aps = {}, []
    for name, v in arrays.items():
        v = np.ascontiguousarray(v)
        ins[f"in_{name}"] = v
        aps.append(nc.dram_tensor(f"in_{name}", v.shape, mybir.dt.from_np(v.dtype), kind="ExternalInput").ap())
    out = nc.dram_tensor("out_h", (NB, NW, C), F32, kind="ExternalOutput").ap()
    build(nc, *aps, out)
    r = run_bass_kernel_spmd(nc, [ins], core_ids=[0])
    return r.results[0]["out_h"]
```
